# Optimizing a Trainium2 kernel written in Bass

```python
import numpy as np
import jax
import jax.numpy as jnp

def _softmax(x, axis=-1):
    return jax.nn.softmax(x, axis=axis)

def _gelu(x):
    return jax.nn.gelu(x, approximate=True)

def _silu(x):
    return jax.nn.silu(x)

def _sigmoid(x):
    return jax.nn.sigmoid(x)

def _layernorm(x, axis=-1, eps=1e-05):
    m = jnp.mean(x, axis=axis, keepdims=True)
    v = jnp.var(x, axis=axis, keepdims=True)
    return (x - m) / jnp.sqrt(v + eps)

def _scatter_add(tgt, idx, src, axis=0):
    return tgt.at[idx].add(src)

def _segment_sum(src, seg, n):
    return jax.ops.segment_sum(src, seg, n)
kernel_name = 'mk_adaln_d2_jaxref_r8_4ce3cd'

def setup_inputs(seed: int=0):
    np.random.seed(seed)
    _w = jnp.asarray

    def _L0_attn_setup():
        import jax, jax.numpy as jnp
        import numpy as np
        BLOCK = 32
        EPS = 1e-06

        def _silu(x):
            return x * jax.nn.sigmoid(x)
        key = jax.random.key(seed)
        k1, k2, k3, k4 = jax.random.split(key, 4)
        embed_dim, hidden_dim = (256, 256)
        b, n, h = (2, 512, 16)
        x = jax.random.normal(k1, (b, n, embed_dim), dtype=jnp.float32)
        slope_rate = jax.random.uniform(k2, (h, 1, 1), dtype=jnp.float32, minval=0.01, maxval=1.0)
        W_qkvu = jax.random.normal(k3, (4 * hidden_dim, embed_dim), dtype=jnp.float32) / np.sqrt(embed_dim)
        W_out = jax.random.normal(k4, (embed_dim, hidden_dim), dtype=jnp.float32) / np.sqrt(hidden_dim)
        return {'x': x, 'slope_rate': slope_rate, 'W_qkvu': W_qkvu, 'W_out': W_out}
    _L0_attn_in = _L0_attn_setup()

    def _L0_ffn_setup():
        import jax, jax.numpy as jnp
        import numpy as np
        TOP_K = 2

        def moe_forward(x, w_gate_router, w_gate_proj, w_up_proj, w_down_proj):
            E = w_gate_router.shape[0]
            scores = jnp.einsum('bsd,ed->bse', x, w_gate_router)
            topk_scores, topk_idx = jax.lax.top_k(scores, TOP_K)
            topk_probs = jax.nn.softmax(topk_scores, axis=-1)
            weights = jnp.sum(topk_probs[..., None] * jax.nn.one_hot(topk_idx, E, dtype=x.dtype), axis=-2)
            gate = jnp.einsum('bsd,efd->bsef', x, w_gate_proj)
            up = jnp.einsum('bsd,efd->bsef', x, w_up_proj)
            hidden = jax.nn.silu(gate) * up
            out = jnp.einsum('bsef,edf,bse->bsd', hidden, w_down_proj, weights)
            return out
        key = jax.random.key(seed)
        k1, k2, k3, k4, k5 = jax.random.split(key, 5)
        B, S, D, E, F = (2, 128, 256, 8, 96)
        scale_in = 1.0 / np.sqrt(D)
        scale_ff = 1.0 / np.sqrt(F)
        return {'x': jax.random.normal(k1, (B, S, D), dtype=jnp.float32), 'w_gate_router': jax.random.normal(k2, (E, D), dtype=jnp.float32) * scale_in, 'w_gate_proj': jax.random.normal(k3, (E, F, D), dtype=jnp.float32) * scale_in, 'w_up_proj': jax.random.normal(k4, (E, F, D), dtype=jnp.float32) * scale_in, 'w_down_proj': jax.random.normal(k5, (E, D, F), dtype=jnp.float32) * scale_ff}
    _L0_ffn_in = _L0_ffn_setup()
    _L0_c = _w((lambda *s: np.random.randn(*s).astype(np.float32) * 0.05)(1, 256))
    _L0_wmod = _w((lambda *s: np.random.randn(*s).astype(np.float32) * 0.05)(256, 6 * 256) * 256 ** (-0.5))

    def _L1_attn_setup():
        import jax, jax.numpy as jnp
        import numpy as np
        key = jax.random.key(seed)
        ks = jax.random.split(key, 5)
        B, S, D = (1, 512, 256)
        H, Dh = (16, 128)
        scale = 1.0 / np.sqrt(D).astype(np.float32)
        return {'x': jax.random.normal(ks[0], (B, S, D), dtype=jnp.float32), 'W_K': jax.random.normal(ks[1], (H, Dh, D), dtype=jnp.float32) * scale, 'W_Q': jax.random.normal(ks[2], (H, Dh, D), dtype=jnp.float32) * scale, 'W_V': jax.random.normal(ks[3], (H, Dh, D), dtype=jnp.float32) * scale, 'W_O': jax.random.normal(ks[4], (D, H * Dh), dtype=jnp.float32) * scale}
    _L1_attn_in = _L1_attn_setup()

    def _L1_ffn_setup():
        import jax, jax.numpy as jnp
        import numpy as np
        H, I, E, TOP_K = (256, 704, 8, 2)

        def _silu_mul_mlp(x, w_gate_up, w_down):
            gu = x @ w_gate_up
            g, u = jnp.split(gu, 2, axis=-1)
            return jax.nn.silu(g) * u @ w_down
        key = jax.random.key(seed)
        ks = jax.random.split(key, 6)
        s = 0.02
        x = jax.random.normal(ks[0], (2, 128, H), jnp.float32)
        gate_w = jax.random.normal(ks[1], (E, H), jnp.float32) * s
        base_gate_up = jax.random.normal(ks[2], (H, 2 * I), jnp.float32) * s
        base_down = jax.random.normal(ks[3], (I, H), jnp.float32) * s
        expert_gate_up = jax.random.normal(ks[4], (E, H, 2 * I), jnp.float32) * s
        expert_down = jax.random.normal(ks[5], (E, I, H), jnp.float32) * s
        return {'x': x, 'gate_w': gate_w, 'base_gate_up': base_gate_up, 'base_down': base_down, 'expert_gate_up': expert_gate_up, 'expert_down': expert_down}
    _L1_ffn_in = _L1_ffn_setup()
    _L1_c = _w((lambda *s: np.random.randn(*s).astype(np.float32) * 0.05)(1, 256))
    _L1_wmod = _w((lambda *s: np.random.randn(*s).astype(np.float32) * 0.05)(256, 6 * 256) * 256 ** (-0.5))
    _d = {'L0_attn_x': _L0_attn_in['x'], 'L0_attn_slope_rate': _L0_attn_in['slope_rate'], 'L0_attn_W_qkvu': _L0_attn_in['W_qkvu'], 'L0_attn_W_out': _L0_attn_in['W_out'], 'L0_ffn_w_gate_router': _L0_ffn_in['w_gate_router'], 'L0_ffn_w_gate_proj': _L0_ffn_in['w_gate_proj'], 'L0_ffn_w_up_proj': _L0_ffn_in['w_up_proj'], 'L0_ffn_w_down_proj': _L0_ffn_in['w_down_proj'], 'L0_c': _L0_c, 'L0_wmod': _L0_wmod, 'L1_attn_W_K': _L1_attn_in['W_K'], 'L1_attn_W_Q': _L1_attn_in['W_Q'], 'L1_attn_W_V': _L1_attn_in['W_V'], 'L1_attn_W_O': _L1_attn_in['W_O'], 'L1_ffn_gate_w': _L1_ffn_in['gate_w'], 'L1_ffn_base_gate_up': _L1_ffn_in['base_gate_up'], 'L1_ffn_base_down': _L1_ffn_in['base_down'], 'L1_ffn_expert_gate_up': _L1_ffn_in['expert_gate_up'], 'L1_ffn_expert_down': _L1_ffn_in['expert_down'], 'L1_c': _L1_c, 'L1_wmod': _L1_wmod}
    _x0 = _d['L0_attn_x']
    _d['L0_attn_x'] = jax.random.normal(jax.random.fold_in(jax.random.key(seed), 1), (1, 2048, 256), dtype=_x0.dtype)
    del _x0
    return _d

def reference(L0_attn_x, L0_attn_slope_rate, L0_attn_W_qkvu, L0_attn_W_out, L0_ffn_w_gate_router, L0_ffn_w_gate_proj, L0_ffn_w_up_proj, L0_ffn_w_down_proj, L0_c, L0_wmod, L1_attn_W_K, L1_attn_W_Q, L1_attn_W_V, L1_attn_W_O, L1_ffn_gate_w, L1_ffn_base_gate_up, L1_ffn_base_down, L1_ffn_expert_gate_up, L1_ffn_expert_down, L1_c, L1_wmod):

    def _L0_attn_ref(x, slope_rate, W_qkvu, W_out):
        import jax, jax.numpy as jnp
        import numpy as np
        BLOCK = 32
        EPS = 1e-06

        def _silu(x):
            return x * jax.nn.sigmoid(x)
        b, n, embed_dim = x.shape
        h = slope_rate.shape[0]
        hidden_dim = W_qkvu.shape[0] // 4
        d = hidden_dim // h
        NB = n // BLOCK
        qkvu = x @ W_qkvu.T
        q, k, v, u = jnp.split(qkvu, 4, axis=-1)

        def to_heads(t):
            return t.reshape(b, n, h, d).transpose(0, 2, 1, 3)
        q = _silu(to_heads(q))
        k = _silu(to_heads(k))
        v = to_heads(v)
        s = slope_rate
        arr = jnp.arange(1, BLOCK + 1, dtype=x.dtype)
        q_decay = jnp.exp(-s * arr[:, None])
        k_decay = jnp.exp(-s * (BLOCK - arr[:, None]))
        idx = arr[:, None] - arr[None, :]
        diag_decay = jnp.exp(jnp.where(idx >= 0, -s * idx, -jnp.inf))
        block_decay = jnp.exp(-s * BLOCK)

        def blk(t):
            return t.reshape(b, h, NB, BLOCK, d).transpose(2, 0, 1, 3, 4)
        qb, kb, vb = (blk(q), blk(k), blk(v))

        def step(kv, inp):
            qi, ki, vi = inp
            qkv_none_diag = jnp.einsum('bhmd,bhde->bhme', qi * q_decay, kv)
            qk = jnp.einsum('bhmd,bhsd->bhms', qi, ki) * diag_decay
            qkv_diag = jnp.einsum('bhms,bhse->bhme', qk, vi)
            kv_new = block_decay * kv + jnp.einsum('bhsd,bhse->bhde', ki * k_decay, vi)
            return (kv_new, qkv_none_diag + qkv_diag)
        kv0 = jnp.zeros((b, h, d, d), dtype=jnp.float32)
        _, outs = jax.lax.scan(step, kv0, (qb, kb, vb))
        o = outs.transpose(1, 2, 0, 3, 4).reshape(b, h, n, d)
        o = o.transpose(0, 2, 1, 3).reshape(b, n, hidden_dim)
        o = o * jax.lax.rsqrt(jnp.mean(o * o, axis=-1, keepdims=True) + EPS)
        o = u * o
        return o @ W_out.T

    def _L0_ffn_ref(x, w_gate_router, w_gate_proj, w_up_proj, w_down_proj):
        import jax, jax.numpy as jnp
        import numpy as np
        TOP_K = 2

        def moe_forward(x, w_gate_router, w_gate_proj, w_up_proj, w_down_proj):
            E = w_gate_router.shape[0]
            scores = jnp.einsum('bsd,ed->bse', x, w_gate_router)
            topk_scores, topk_idx = jax.lax.top_k(scores, TOP_K)
            topk_probs = jax.nn.softmax(topk_scores, axis=-1)
            weights = jnp.sum(topk_probs[..., None] * jax.nn.one_hot(topk_idx, E, dtype=x.dtype), axis=-2)
            gate = jnp.einsum('bsd,efd->bsef', x, w_gate_proj)
            up = jnp.einsum('bsd,efd->bsef', x, w_up_proj)
            hidden = jax.nn.silu(gate) * up
            out = jnp.einsum('bsef,edf,bse->bsd', hidden, w_down_proj, weights)
            return out
        return moe_forward(x, w_gate_router, w_gate_proj, w_up_proj, w_down_proj)

    def _L1_attn_ref(x, W_K, W_Q, W_V, W_O):
        import jax, jax.numpy as jnp
        import numpy as np
        b, pos, d_model = x.shape
        d_head = W_K.shape[1]
        k = jnp.einsum('ihd,bpd->biph', W_K, x)
        q = jnp.einsum('ihd,bpd->biph', W_Q, x)
        v = jnp.einsum('ihd,bpd->biph', W_V, x)
        scores = jnp.einsum('biph,biqh->biqp', k, q)
        mask = jnp.tril(jnp.ones((pos, pos), dtype=x.dtype))
        masked = scores * mask - jnp.float32(10000000000.0) * (1.0 - mask)
        attn = jax.nn.softmax(masked / jnp.sqrt(jnp.float32(d_head)), axis=-1)
        z = jnp.einsum('biqp,biph->biqh', attn, v)
        z_flat = jnp.transpose(z, (0, 2, 1, 3)).reshape(b, pos, -1)
        out = jnp.einsum('df,bqf->bqd', W_O, z_flat)
        return out

    def _L1_ffn_ref(x, gate_w, base_gate_up, base_down, expert_gate_up, expert_down):
        import jax, jax.numpy as jnp
        import numpy as np
        H, I, E, TOP_K = (256, 704, 8, 2)

        def _silu_mul_mlp(x, w_gate_up, w_down):
            gu = x @ w_gate_up
            g, u = jnp.split(gu, 2, axis=-1)
            return jax.nn.silu(g) * u @ w_down
        B, S, Hd = x.shape
        xt = x.reshape(-1, Hd)
        base_y = _silu_mul_mlp(xt, base_gate_up, base_down)
        logits = xt @ gate_w.T
        rw = jax.nn.softmax(logits.astype(jnp.float32), axis=-1)
        top_w, top_e = jax.lax.top_k(rw, TOP_K)
        top_w = top_w / top_w.sum(axis=-1, keepdims=True)
        top_w = top_w.astype(x.dtype)
        combine = (jax.nn.one_hot(top_e, E, dtype=x.dtype) * top_w[..., None]).sum(1)
        gu = jnp.einsum('th,ehi->eti', xt, expert_gate_up)
        g, u = jnp.split(gu, 2, axis=-1)
        act = jax.nn.silu(g) * u
        out = jnp.einsum('eti,eih->eth', act, expert_down)
        moe_y = jnp.einsum('eth,te->th', out, combine)
        return (moe_y + base_y).reshape(B, S, Hd)
    x = L0_attn_x
    mod = (_silu(L0_c) @ L0_wmod).reshape(L0_c.shape[0], 6, 1, -1)
    sa, ca, ga, sb, cb, gb = (mod[:, 0], mod[:, 1], mod[:, 2], mod[:, 3], mod[:, 4], mod[:, 5])
    ga = (2 * (ga >= 0) - 1) * jnp.maximum(jnp.abs(ga), 0.25)
    gb = (2 * (gb >= 0) - 1) * jnp.maximum(jnp.abs(gb), 0.25)
    h = _layernorm(x, axis=-1) * (1 + ca) + sa
    x = x + ga * _L0_attn_ref(h, L0_attn_slope_rate, L0_attn_W_qkvu, L0_attn_W_out)
    h = _layernorm(x, axis=-1) * (1 + cb) + sb
    x = x + gb * _L0_ffn_ref(h, L0_ffn_w_gate_router, L0_ffn_w_gate_proj, L0_ffn_w_up_proj, L0_ffn_w_down_proj)
    mod = (_silu(L1_c) @ L1_wmod).reshape(L1_c.shape[0], 6, 1, -1)
    sa, ca, ga, sb, cb, gb = (mod[:, 0], mod[:, 1], mod[:, 2], mod[:, 3], mod[:, 4], mod[:, 5])
    ga = (2 * (ga >= 0) - 1) * jnp.maximum(jnp.abs(ga), 0.25)
    gb = (2 * (gb >= 0) - 1) * jnp.maximum(jnp.abs(gb), 0.25)
    h = _layernorm(x, axis=-1) * (1 + ca) + sa
    x = x + ga * _L1_attn_ref(h, L1_attn_W_K, L1_attn_W_Q, L1_attn_W_V, L1_attn_W_O)
    h = _layernorm(x, axis=-1) * (1 + cb) + sb
    x = x + gb * _L1_ffn_ref(h, L1_ffn_gate_w, L1_ffn_base_gate_up, L1_ffn_base_down, L1_ffn_expert_gate_up, L1_ffn_expert_down)
    return x

_drawn_inputs = setup_inputs


def setup_inputs(seed=0):
    import zlib

    import numpy as np

    out = dict(_drawn_inputs(seed))
    spreads = {}
    factors = {'L1_ffn_gate_w': 8.0,
     'L1_ffn_base_gate_up': 8.0,
     'L1_ffn_base_down': 8.0,
     'L1_ffn_expert_gate_up': 8.0,
     'L1_ffn_expert_down': 8.0}
    for name, (base, spread) in spreads.items():
        noise = np.random.default_rng([zlib.crc32(name.encode()), seed]).standard_normal(out[name].shape)
        drawn = base * np.exp(spread * noise) if base else spread * noise
        out[name] = jnp.asarray(drawn.astype(out[name].dtype))
    for name, factor in factors.items():
        out[name] = (out[name] * factor).astype(out[name].dtype)
    return out
```

```python
from contextlib import ExitStack

import concourse.bass as bass
from concourse import mybir

F32 = mybir.dt.float32
F32R = mybir.dt.float32r
I32 = mybir.dt.int32
ALU = mybir.AluOpType
ACT = mybir.ActivationFunctionType
AX = mybir.AxisListType

P = 128
LN_EPS = 1e-5
RMS_EPS = 1e-6
LEAST_GATE = 0.25
MASKED = -1e10
LOWEST = -3.0e38


class Turn:

    def __init__(self):
        self.fixed, self.round = 0, None

    def at(self):
        return self.fixed if self.round is None else self.fixed + self.round

    def next(self):
        at = self.at()
        self.fixed += 1
        return at

    def enter(self, i, per):
        self.round, self.start, self.per = i * per, self.fixed, per

    def leave(self, rounds):
        assert self.fixed == self.start + self.per, (self.fixed, self.start, self.per)
        self.fixed, self.round = self.start + self.per * rounds, None


def wait(eng, sem, value):
    if isinstance(value, int) and value <= 0:
        return
    eng.wait_ge(sem, value)


def two_blocks(nc, x_in, slope, w_qk, w_kvu, w_out0, router0, gu0, down0, c0, wmod0,
               w_k, w_q, w_v, w_o, router1, gu1, down1, c1, wmod1, out, stop=9):
    S, D = x_in.shape
    NT = S // P
    KB = D // P
    CH = 512
    NC_ = S // CH
    TC = CH // P
    H0 = slope.shape[0]
    D0 = D // H0
    STRIP = 32
    HG = P // STRIP
    G0 = H0 // HG
    H1, _, DH = w_k.shape
    E = router0.shape[1]

    ctx = ExitStack()
    with ctx:
        def sem(name):
            return ctx.enter_context(nc.semaphore(name))

        def sb(name, shape, dt=F32, where=ctx):
            return where.enter_context(nc.sbuf_tensor(name, shape, dt))

        bank = [ctx.enter_context(nc.psum_tensor(f"bank{n}", [P, 512], F32)) for n in range(8)]
        WORK, SIDE = 4, 4

        x = sb("x", [P, NT, D])
        h_hi = sb("h_hi", [P, KB, S], F32R)
        h_lo = sb("h_lo", [P, KB, S], F32R)
        ident = sb("ident", [P, P])
        one = sb("one", [P, 1])
        spare = sb("spare", [P, 1])
        eps_ln = sb("eps_ln", [P, 1])
        eps_rms = sb("eps_rms", [P, 1])
        cols = [sb(f"cols{n}", [P, 4, KB]) for n in range(2)]
        gates = [sb(f"gates{n}", [P, 2, D]) for n in range(2)]
        stats = sb("stats", [P, NT, 6])
        msum = sb("msum", [P, NT])
        mdif = sb("mdif", [P, NT])
        vsum = sb("vsum", [P, NT])
        rstd = sb("rstd", [P, NT])
        comb = sb("comb", [P, NT, E + 1])

        def norm_buffers(where, tag):
            return (sb(f"xhat{tag}", [P, 2 * TC, D], where=where), sb(f"hf{tag}", [P, 4, CH], where=where))

        st = ExitStack()
        wmod = sb("wmod", [P, KB, 6 * D], where=st)
        cin = sb("cin", [P, KB], where=st)
        csil = sb("csil", [P, KB], where=st)
        cwide = sb("cwide", [P, KB, P], where=st)
        gabs = sb("gabs", [P, 2, D], where=st)
        gsgn = sb("gsgn", [P, 2, D], where=st)
        ones = sb("ones", [P, P], where=st)

        wqk = sb("wqk", [P, KB, 2 * D], where=st)
        wqk_hi = sb("wqk_hi", [P, KB, 2 * G0, P], F32R, where=st)
        wqk_lo = sb("wqk_lo", [P, KB, 2 * G0, P], F32R, where=st)
        wkvu = sb("wkvu", [P, KB, 3 * D], where=st)
        wkvu_hi = sb("wkvu_hi", [P, KB, 3 * D], F32R, where=st)
        wkvu_lo = sb("wkvu_lo", [P, KB, 3 * D], F32R, where=st)
        wo0 = sb("wo0", [P, KB, D], where=st)
        wo0_hi = sb("wo0_hi", [P, KB, D], F32R, where=st)
        wo0_lo = sb("wo0_lo", [P, KB, D], F32R, where=st)
        hc_hi = sb("hc_hi", [P, KB, CH], F32R, where=st)
        hc_lo = sb("hc_lo", [P, KB, CH], F32R, where=st)
        nslope = sb("nslope", [P, H0], where=st)
        nslope_s = sb("nslope_s", [P, G0], where=st)
        lag_i = sb("lag_i", [P, P], I32, where=st)
        lag = sb("lag", [P, P], where=st)
        rowi = sb("rowi", [P, P], I32, where=st)
        rowf = sb("rowf", [P, P], where=st)
        endi = sb("endi", [P, 1], I32, where=st)
        endf = sb("endf", [P, 1], where=st)
        decay = sb("decay", [P, HG, G0, P], where=st)
        qdec = sb("qdec", [P, G0, P], where=st)
        kdec = sb("kdec", [P, H0], where=st)
        bdec = sb("bdec", [P, G0], where=st)
        own = sb("own", [P, HG, D0], where=st)
        qT = sb("qT", [P, G0, CH], where=st)
        kT = sb("kT", [P, G0, CH], where=st)
        qdT = sb("qdT", [P, G0, CH], where=st)
        ksil = sb("ksil", [P, 2, D], where=st)
        kd = sb("kd", [P, 2, H0, STRIP], where=st)
        vt = sb("vt", [P, 2, D], where=st)
        ut = sb("ut", [P, 2, D], where=st)
        amat = sb("amat", [P, HG, G0, P], where=st)
        kv = sb("kv", [P, G0, HG * D0], where=st)
        kvn = sb("kvn", [P, G0, HG * D0], where=st)
        ou = sb("ou", [P, 2, D], where=st)
        osq = sb("osq", [P, D], where=st)
        ssq = sb("ssq", [P, TC], where=st)
        rms = sb("rms", [P, TC], where=st)
        oT_hi = sb("oT_hi", [P, TC, D], F32R, where=st)
        oT_lo = sb("oT_lo", [P, TC, D], F32R, where=st)
        xhat, hf = norm_buffers(st, "a")
        st.close()

        st = ExitStack()
        F_L = [down0.shape[1], down1.shape[1]]
        FT = -(-F_L[1] // P)
        FMAX = F_L[1]
        mgu = sb("mgu", [P, KB, 2 * FMAX], where=st)
        mdn = sb("mdn", [P, FT, D], where=st)
        gu_hi = [sb(f"gu_hi{n}", [P, KB, 2 * FMAX], F32R, where=st) for n in range(2)]
        gu_lo = [sb(f"gu_lo{n}", [P, KB, 2 * FMAX], F32R, where=st) for n in range(2)]
        dn_hi = [sb(f"dn_hi{n}", [P, FT, D], F32R, where=st) for n in range(2)]
        dn_lo = [sb(f"dn_lo{n}", [P, FT, D], F32R, where=st) for n in range(2)]
        HID = 8
        hid_hi = sb("hid_hi", [P, HID, CH], F32R, where=st)
        hid_lo = sb("hid_lo", [P, HID, CH], F32R, where=st)
        sil = sb("sil", [P, 2, CH], where=st)
        hid = sb("hid", [P, 2, CH], where=st)
        rt = sb("rt", [P, KB, E], where=st)
        rt_hi = sb("rt_hi", [P, KB, E], F32R, where=st)
        rt_lo = sb("rt_lo", [P, KB, E], F32R, where=st)
        low = sb("low", [P, E, E], where=st)
        sc = sb("sc", [P, NT, E], where=st)
        rank = sb("rank", [P, NT, E], where=st)
        top = sb("top", [P, NT], where=st)
        den = sb("den", [P, NT], where=st)
        xhat_m, hf_m = norm_buffers(st, "m")
        gt = hf_m[:, 0:2, :].rearrange("p a (t e f) -> p (a t) e f", e=E, f=E)
        eq = hf_m[:, 2:4, :].rearrange("p a (t e f) -> p (a t) e f", e=E, f=E)
        st.close()

        st = ExitStack()
        KT_hi = sb("KT_hi", [P, S], F32R, where=st)
        KT_lo = sb("KT_lo", [P, S], F32R, where=st)
        QT_hi = sb("QT_hi", [P, 2, CH], F32R, where=st)
        QT_lo = sb("QT_lo", [P, 2, CH], F32R, where=st)
        V_hi = sb("V_hi", [P, NT, 2 * DH], F32R, where=st)
        V_lo = sb("V_lo", [P, NT, 2 * DH], F32R, where=st)
        SLOT = 4
        def row_width(q, r):
            return (q * TC + r + 1) * P

        def row_start(q, r):
            return sum(row_width(NC_ - 2 + q % 2, a) + SLOT for a in range(r))

        prob = [sb(f"prob{n}", [P, row_start(n, TC)], where=st) for n in range(2)]
        PTR = 4
        pT_hi = sb("pT_hi", [P, PTR, CH], F32R, where=st)
        pT_lo = sb("pT_lo", [P, PTR, CH], F32R, where=st)
        zT_hi = sb("zT_hi", [P, CH], F32R, where=st)
        zT_lo = sb("zT_lo", [P, CH], F32R, where=st)
        wkq = sb("wkq", [P, KB, 4 * DH], where=st)
        wkq_hi = sb("wkq_hi", [P, KB, 4 * DH], F32R, where=st)
        wkq_lo = sb("wkq_lo", [P, KB, 4 * DH], F32R, where=st)
        wv = sb("wv", [P, KB, 2 * DH], where=st)
        wv_hi = sb("wv_hi", [P, KB, 2 * DH], F32R, where=st)
        wv_lo = sb("wv_lo", [P, KB, 2 * DH], F32R, where=st)
        wo = sb("wo", [P, 2, D], where=st)
        wo_hi = sb("wo_hi", [P, 2, D], F32R, where=st)
        wo_lo = sb("wo_lo", [P, 2, D], F32R, where=st)
        negmask = sb("negmask", [P, P], where=st)
        nmax = sb("nmax", [P, NC_, TC], where=st)
        rsum = sb("rsum", [P, NC_, TC], where=st)
        rinv = sb("rinv", [P, NC_, TC], where=st)
        xhat_s = prob[1][:, 0:8 * D].rearrange("p (t d) -> p t d", d=D)
        hf_s = prob[1][:, 8 * D:8 * D + 4 * CH].rearrange("p (t d) -> p t d", d=CH)
        st.close()

        work_full = sem("work_full")
        work_free = sem("work_free")
        x_loaded = [sem(f"x_loaded{c}") for c in range(NC_)]
        consts = sem("consts")
        c_loaded = sem("c_loaded")
        wmod_loaded = sem("wmod_loaded")
        c_silu = sem("c_silu")
        c_wide = sem("c_wide")
        mod_step = sem("mod_step")
        n_step = [sem(f"n_step{n}") for n in range(4)]
        n_std = [sem(f"n_std{n}") for n in range(4)]
        n_xhat = [sem(f"n_xhat{n}") for n in range(4)]
        n_hi = [sem(f"n_hi{n}") for n in range(4)]
        n_lo = [sem(f"n_lo{n}") for n in range(4)]
        x_done = [sem(f"x_done{n}") for n in range(4)]
        a_loaded = [sem(f"a_loaded{n}") for n in range(5)]
        a_split = sem("a_split")
        a_tab = sem("a_tab")
        a_exp = sem("a_exp")
        a_sel = sem("a_sel")
        a_hc = sem("a_hc")
        a_silu = sem("a_silu")
        a_ks = sem("a_ks")
        a_kd = sem("a_kd")
        a_score = sem("a_score")
        a_mask = sem("a_mask")
        a_sq = sem("a_sq")
        a_kv = sem("a_kv")
        a_std = sem("a_std")
        a_rms = sem("a_rms")
        a_ohi = sem("a_ohi")
        m_rt = [sem(f"m_rt{n}") for n in range(2)]
        m_gu = [sem(f"m_gu{n}") for n in range(2)]
        m_dn = [sem(f"m_dn{n}") for n in range(2)]
        m_raw = [sem(f"m_raw{n}") for n in range(2)]
        m_zero = sem("m_zero")
        m_top = [sem(f"m_top{n}") for n in range(2)]
        m_sc = [sem(f"m_sc{n}") for n in range(2)]
        m_exp = [sem(f"m_exp{n}") for n in range(2)]
        m_sil = [sem(f"m_sil{n}") for n in range(2)]
        m_hi = [sem(f"m_hi{n}") for n in range(2)]
        m_lo = [sem(f"m_lo{n}") for n in range(2)]
        m_y = [sem(f"m_y{n}") for n in range(2)]
        s_w = sem("s_w")
        s_split = sem("s_split")
        s_neg = sem("s_neg")
        s_full = sem("s_full")
        s_free = sem("s_free")
        s_hi = sem("s_hi")
        s_row = sem("s_row")
        s_exp = sem("s_exp")
        s_pt = sem("s_pt")
        s_phi = sem("s_phi")
        s_plo = sem("s_plo")
        s_z = sem("s_z")
        s_zhi = sem("s_zhi")
        s_zlo = sem("s_zlo")
        s_inv = sem("s_inv")
        stored = sem("stored")

        block = ctx.enter_context(nc.Block())

        def mo(n):
            return ((xhat, hf), (xhat_m, hf_m), (xhat_s, hf_s), (xhat_m, hf_m))[n]

        XD = [1 + NT * a for a in (1, gu0.shape[0], H1, gu1.shape[0])]
        A_EXPS = H0 + G0 + 2
        A_BASE = 2 * 2 + NC_ * KB
        A_WORK = 2 * G0 + 6 * TC
        S_RING = 3
        HEAD_WORK = 2 * NC_ + TC * sum(range(1, NC_ + 1)) + NT // 2
        PAIR_WORK = NT // 2 + 2 * HEAD_WORK
        PAIR_SPLIT, PAIR_LOADS = 10, 7 * 16
        HEAD_PT = sum(TC * (q + 1) for q in range(NC_))
        Z_BANK = 7
        ORDER = [("K", 0, 0), ("Q", 0, 0), ("Q", 0, 1), ("V", 0, 0), ("S", 0, 0), ("Q", 0, 2), ("S", 0, 1),
                 ("Q", 0, 3), ("T", 0, 0), ("S", 0, 2), ("O", 0, 0), ("T", 0, 1), ("S", 0, 3), ("O", 0, 1),
                 ("T", 0, 2), ("K", 1, 0), ("Q", 1, 0), ("Q", 1, 1), ("O", 0, 2), ("T", 0, 3),
                 ("S", 1, 0), ("Q", 1, 2), ("O", 0, 3), ("S", 1, 1), ("Q", 1, 3),
                 ("T", 1, 0), ("S", 1, 2), ("O", 1, 0), ("T", 1, 1), ("S", 1, 3), ("O", 1, 1),
                 ("T", 1, 2), ("O", 1, 2), ("T", 1, 3), ("O", 1, 3)]

        ROWS_BY = {}
        for what, j, q in ORDER:
            if what == "S":
                ROWS_BY[j, q] = TC * (len(ROWS_BY) + 1)

        def work_of(what, q):
            return {"K": NC_, "Q": 1, "V": NT // 2, "S": TC * (q + 1), "T": 0, "O": TC // 2}[what]

        def work_behind(n):
            return sum(work_of(what, q) for what, _, q in ORDER[:n])

        assert work_behind(len(ORDER)) == PAIR_WORK and PAIR_WORK % S_RING == 0 and 2 * HEAD_PT % 4 == 0
        m_tiles = [[(f * P, min(P, F - f * P)) for f in range(-(-F // P))] for F in F_L]
        m_count = [gu0.shape[0], gu1.shape[0]]
        m_base = [A_BASE + NC_ * A_WORK + NC_ * KB]
        m_base.append(m_base[0] + m_count[0] * 2 * len(m_tiles[0]) * NC_ + 2 * NC_ * KB)

        @block.sync
        def _(sp):
            sp.dma_start(cin[:, :], c0).then_inc(c_loaded, 16)
            sp.dma_start(wmod[:, :, :], wmod0.rearrange("(k p) n -> p k n", p=P)).then_inc(wmod_loaded, 16)
            for c in range(NC_):
                sp.dma_start(x[:, c * TC:(c + 1) * TC, :],
                             x_in[c * CH:(c + 1) * CH, :].rearrange("(t p) d -> p t d", p=P)).then_inc(x_loaded[c], 16)
            sp.dma_start(nslope[:, :], slope.rearrange("h a b -> (a b) h").to_broadcast([P, H0])).then_inc(a_loaded[3], 16)
            with nc.allow_non_contiguous_dma(reason="one slope for each strip"):
                for r in range(HG):
                    sp.dma_start(nslope_s[r * STRIP:(r + 1) * STRIP, :],
                                 slope[r::HG].rearrange("h a b -> (a b) h").to_broadcast([STRIP, G0])).then_inc(a_loaded[4], 16)
            sp.dma_start(wqk[:, :, :], w_qk.rearrange("(k p) n -> p k n", p=P)).then_inc(a_loaded[0], 16)
            sp.dma_start(wkvu[:, :, :], w_kvu.rearrange("(k p) n -> p k n", p=P)).then_inc(a_loaded[1], 16)
            sp.dma_start(wo0[:, :, :], w_out0.rearrange("(k p) n -> p k n", p=P)).then_inc(a_loaded[2], 16)
            sp.wait_ge(mod_step, 5)
            sp.dma_start(cin[:, :], c1).then_inc(c_loaded, 16)
            sp.dma_start(wmod[:, :, :], wmod1.rearrange("(k p) n -> p k n", p=P)).then_inc(wmod_loaded, 16)

            def load_expert(n, e, before, before_dn):
                gu, dn, F = (gu0, gu1)[n], (down0, down1)[n], F_L[n]
                wait(sp, m_raw[n], before)
                sp.dma_start(mgu[:, :, 0:2 * F], gu[bass.ds(e, 1), :, :].rearrange("a (k p) f -> p (a k) f", p=P)).then_inc(m_gu[n], 16)
                wait(sp, m_raw[n], before_dn)
                full = F // P
                if full:
                    sp.dma_start(mdn[:, 0:full, :], dn[bass.ds(e, 1), 0:full * P, :].rearrange("a (f p) d -> p (a f) d", p=P)).then_inc(m_dn[n], 16)
                sp.dma_start(mdn[0:F - full * P, full, :], dn[bass.ds(e, 1), full * P:F, :].rearrange("a p d -> (a p) d")).then_inc(m_dn[n], 16)

            def mixture(n):
                router = (router0, router1)[n]
                sp.wait_ge(x_done[2 * n], XD[2 * n])
                sp.dma_start(rt[:, :, :], router.rearrange("(k p) e -> p k e", p=P)).then_inc(m_rt[n], 16)
                sp.wait_ge(n_lo[2 * n + 1], NC_ * KB)
                load_expert(n, 0, 0, 0)
                rounds = (m_count[n] - 1) // 2
                with sp.Fori(0, rounds) as i:
                    for half in range(2):
                        load_expert(n, 2 * i + half + 1, i * 10 + 5 * half + 2, i * 10 + 5 * half + 5)
                if m_count[n] - 2 * rounds == 2:
                    load_expert(n, m_count[n] - 1, 10 * rounds + 2, 10 * rounds + 5)

            if stop >= 1:
                mixture(0)
            if stop >= 2:
                sp.wait_ge(x_done[1], XD[1])
                def load_pair(i):
                    for j in range(2):
                        for a, w in enumerate((w_k, w_q)):
                            sp.dma_start(wkq[:, :, (2 * j + a) * DH:(2 * j + a + 1) * DH],
                                         w[bass.ds(2 * i + j, 1), :, :].rearrange("a (k p) h -> p (a k) h", p=P)).then_inc(s_w, 16)
                        sp.dma_start(wv[:, :, j * DH:(j + 1) * DH],
                                     w_v[bass.ds(2 * i + j, 1), :, :].rearrange("a (k p) h -> p (a k) h", p=P)).then_inc(s_w, 16)
                    sp.dma_start(wo[:, :, :], w_o[bass.ds(2 * i, 2), :, :].rearrange("a p d -> p a d")).then_inc(s_w, 16)

                load_pair(0)
                with sp.Fori(0, H1 // 2 - 1) as i:
                    sp.wait_ge(s_split, i * PAIR_SPLIT + PAIR_SPLIT)
                    load_pair(i + 1)
            if stop >= 3:
                mixture(1)
            last = min(stop, 3)
            sp.wait_ge(x_done[last], XD[last])
            for c in range(NC_):
                sp.dma_start(out[c * CH:(c + 1) * CH, :].rearrange("(t p) d -> p t d", p=P),
                             x[:, c * TC:(c + 1) * TC, :]).then_inc(stored, 16)
            sp.wait_ge(stored, 16 * NC_)

        @block.gpsimd
        def _(pool):
            def rounded(out_, in_):
                ones_ = one[:, :].rearrange("p (a b) -> p a b", a=1).to_broadcast(list(in_.shape))
                return pool.tensor_tensor(out_, in_, ones_, ALU.mult)

            pool.memset(ident[:, :], 0.0).then_inc(consts, 1)
            pool.memset(ones[:, :], 1.0).then_inc(consts, 1)
            pool.memset(eps_ln[:, :], LN_EPS).then_inc(consts, 1)
            pool.memset(eps_rms[:, :], RMS_EPS).then_inc(consts, 1)
            pool.memset(one[:, :], 1.0).then_inc(a_split, 1)
            pool.wait_ge(consts, 4)
            pool.affine_select(out=ident[:, :], in_=ident[:, :], compare_op=ALU.not_equal, fill=1.0,
                               base=0, pattern=[[-1, P]], channel_multiplier=1).then_inc(consts, 1)
            pool.iota(lag_i[:, :], pattern=[[1, P]], base=0, channel_multiplier=-1).then_inc(consts, 1)
            pool.iota(rowi[:, :], pattern=[[1, P]], base=1, channel_multiplier=0).then_inc(consts, 1)
            pool.iota(endi[:, :], pattern=[[0, 1]], base=P - 1, channel_multiplier=-1).then_inc(consts, 1)
            pool.memset(own[:, :, :], 1.0).then_inc(consts, 1)
            pool.wait_ge(consts, 9)
            pool.affine_select(out=own[:, :, :], in_=own[:, :, :], compare_op=ALU.is_ge, fill=0.0,
                               base=0, pattern=[[-STRIP, HG], [0, D0]], channel_multiplier=1).then_inc(consts, 1)
            pool.wait_ge(consts, 10)
            pool.affine_select(out=own[:, :, :], in_=own[:, :, :], compare_op=ALU.is_ge, fill=0.0,
                               base=D0 - 1, pattern=[[STRIP, HG], [0, D0]], channel_multiplier=-1).then_inc(consts, 1)
            for t in (wqk_hi, wqk_lo):
                pool.memset(t[:, :, :, :].bitcast(F32), 0.0).then_inc(a_split, 1)
            pool.memset(kd[:, :, :, :], 0.0).then_inc(a_sel, 1)
            pool.wait_ge(a_split, 3)
            pool.wait_ge(a_loaded[0], 16)
            for k in range(KB):
                raw = wqk[:, k, :].rearrange("p (g r d) -> p g r d", r=HG, d=D0)
                hi = wqk_hi[:, k, :, :].rearrange("p g (r s) -> p g r s", s=STRIP)[:, :, :, 0:D0]
                lo = wqk_lo[:, k, :, :].rearrange("p g (r s) -> p g r s", s=STRIP)[:, :, :, 0:D0]
                pool.tensor_copy(hi, raw).then_inc(a_split, 1)
                pool.wait_ge(a_split, 4 + 2 * k)
                pool.tensor_tensor(lo, raw, hi.bitcast(F32), ALU.subtract).then_inc(a_split, 1)
            pool.wait_ge(a_loaded[1], 16)
            pool.tensor_copy(wkvu_hi[:, :, :], wkvu[:, :, :]).then_inc(a_split, 1)
            pool.wait_ge(a_split, 8)
            pool.tensor_tensor(wkvu_lo[:, :, :], wkvu[:, :, :], wkvu_hi[:, :, :].bitcast(F32), ALU.subtract).then_inc(a_split, 1)
            pool.wait_ge(a_loaded[2], 16)
            pool.wait_ge(mod_step, 5)
            for k in range(KB):
                pool.tensor_tensor(wo0[:, k, :], wo0[:, k, :], gates[0][:, 0, :], ALU.mult).then_inc(a_split, 1)
            pool.wait_ge(a_split, 11)
            pool.tensor_copy(wo0_hi[:, :, :], wo0[:, :, :]).then_inc(a_split, 1)
            pool.wait_ge(a_split, 12)
            pool.tensor_tensor(wo0_lo[:, :, :], wo0[:, :, :], wo0_hi[:, :, :].bitcast(F32), ALU.subtract).then_inc(a_split, 1)
            pool.wait_ge(a_exp, H0)
            pool.affine_select(out=decay[:, :, :, :].rearrange("p r g m -> p (r g) m"),
                               in_=decay[:, :, :, :].rearrange("p r g m -> p (r g) m"),
                               compare_op=ALU.is_ge, fill=0.0, base=0,
                               pattern=[[0, H0], [1, P]], channel_multiplier=-1).then_inc(a_sel, 1)
            with pool.Fori(0, NC_) as i:
                pool.wait_ge(n_lo[0], KB * i + KB)
                pool.wait_ge(work_full, A_BASE + i * A_WORK)
                for k in range(KB):
                    pool.tensor_copy(hc_hi[:, k, :], h_hi[:, k, bass.ds(i * CH, CH)]).then_inc(a_hc, 1)
                    pool.tensor_copy(hc_lo[:, k, :], h_lo[:, k, bass.ds(i * CH, CH)]).then_inc(a_hc, 1)

            def split_expert(n, half, at, loads):
                F, tiles = F_L[n], m_tiles[n]
                nt, dmas = len(tiles), 1 + (F_L[n] >= P)
                pool.wait_ge(m_gu[n], loads * 16)
                rounded(gu_hi[half][:, :, 0:2 * F], mgu[:, :, 0:2 * F]).then_inc(m_raw[n], 1)
                pool.wait_ge(m_raw[n], at + 1)
                pool.tensor_tensor(gu_lo[half][:, :, 0:2 * F], mgu[:, :, 0:2 * F],
                                   gu_hi[half][:, :, 0:2 * F].bitcast(F32), ALU.subtract).then_inc(m_raw[n], 1)
                pool.wait_ge(m_dn[n], loads * 16 * dmas)
                pool.wait_ge(m_raw[n], at + 2)
                pool.tensor_tensor(mdn[:, 0:nt, :], mdn[:, 0:nt, :],
                                   gates[n][:, 1:2, :].to_broadcast([P, nt, D]), ALU.mult).then_inc(m_raw[n], 1)
                pool.wait_ge(m_raw[n], at + 3)
                rounded(dn_hi[half][:, 0:nt, :], mdn[:, 0:nt, :]).then_inc(m_raw[n], 1)
                pool.wait_ge(m_raw[n], at + 4)
                pool.tensor_tensor(dn_lo[half][:, 0:nt, :], mdn[:, 0:nt, :],
                                   dn_hi[half][:, 0:nt, :].bitcast(F32), ALU.subtract).then_inc(m_raw[n], 1)

            def mixture(n):
                pool.wait_ge(x_done[2 * n], XD[2 * n])
                F, tiles = F_L[n], m_tiles[n]
                last = len(tiles) - 1
                pad = tiles[-1][1]
                zeroed = 5 * n
                pool.memset(low[:, :, :], 1.0).then_inc(m_zero, 1)
                for b in (mdn[pad:P, last, :], hid_hi[pad:P, :, :].bitcast(F32), hid_lo[pad:P, :, :].bitcast(F32)):
                    zeroed += 1
                    pool.wait_ge(m_zero, zeroed)
                    pool.memset(b, 0.0).then_inc(m_zero, 1)
                pool.wait_ge(m_zero, zeroed + 1)
                pool.affine_select(out=low[:, :, :], in_=low[:, :, :], compare_op=ALU.is_gt, fill=0.0,
                                   base=0, pattern=[[1, E], [-1, E]], channel_multiplier=0).then_inc(m_zero, 1)
                pool.wait_ge(m_zero, zeroed + 2)
                split_expert(n, 0, 0, 1)
                T = m_count[n]
                rounds = (T - 1) // 2
                uses = 2 * len(tiles) * NC_
                begun = m_base[n] + 1
                with pool.Fori(0, rounds) as i:
                    pool.wait_ge(work_full, i * 2 * uses + begun)
                    split_expert(n, 1, i * 10 + 5, 2 * i + 2)
                    pool.wait_ge(work_full, i * 2 * uses + begun + uses)
                    split_expert(n, 0, i * 10 + 10, 2 * i + 3)
                if T - 2 * rounds == 2:
                    pool.wait_ge(work_full, rounds * 2 * uses + begun)
                    split_expert(n, 1, rounds * 10 + 5, T)

            if stop >= 1:
                mixture(0)
            if stop >= 2:
                pool.wait_ge(x_done[1], XD[1])
                pool.memset(negmask[:, :], 0.0).then_inc(s_neg, 1)
                pool.wait_ge(s_neg, 1)
                pool.affine_select(out=negmask[:, :], in_=negmask[:, :], compare_op=ALU.is_ge, fill=MASKED,
                                   base=0, pattern=[[-1, P]], channel_multiplier=1).then_inc(s_neg, 1)
                after = {(what, j, q): work_behind(n + 1) for n, (what, j, q) in enumerate(ORDER)}

                def split_pair(pair, used):
                    at = pair * PAIR_SPLIT
                    pool.wait_ge(s_w, pair * PAIR_LOADS + PAIR_LOADS)

                    def split(hi, lo, raw, step):
                        rounded(hi, raw).then_inc(s_split, 1)
                        pool.wait_ge(s_split, at + step + 1)
                        pool.tensor_tensor(lo, raw, hi.bitcast(F32), ALU.subtract).then_inc(s_split, 1)

                    used(after["V", 0, 0])
                    split(wv_hi[:, :, :], wv_lo[:, :, :], wv[:, :, :], 0)
                    for j in range(2):
                        used(after["Q", j, NC_ - 1])
                        c = slice(2 * j * DH, (2 * j + 2) * DH)
                        split(wkq_hi[:, :, c], wkq_lo[:, :, c], wkq[:, :, c], 2 + 2 * j)
                    for j in range(2):
                        pool.tensor_tensor(wo[:, j, :], wo[:, j, :], gates[1][:, 0, :], ALU.mult).then_inc(s_split, 1)
                    pool.wait_ge(s_split, at + 8)
                    used(PAIR_WORK)
                    split(wo_hi[:, :, :], wo_lo[:, :, :], wo[:, :, :], 8)

                split_pair(0, lambda work: None)
                with pool.Fori(0, H1 // 2 - 1) as i:
                    split_pair(i + 1, lambda work: pool.wait_ge(s_full, i * PAIR_WORK + work))
            if stop >= 3:
                mixture(1)

        @block.vector
        def _(dve):
            work = Turn()

            for n in range(2):
                dve.wait_ge(c_silu, n + 1)
                dve.wait_ge(consts, 2)
                if n:
                    dve.wait_ge(work_full, 2)
                for k in range(KB):
                    dve.tensor_scalar(cwide[:, k, :], ones[:, :], csil[:, k:k + 1], None, ALU.mult).then_inc(c_wide, 1)
                at = work.next()
                dve.wait_ge(work_full, at + 1)
                dve.tensor_copy(cols[n][:, :, :].rearrange("p v k -> p (v k)"), bank[at % WORK][:, 0:4 * KB]).then_inc(work_free, 1)
                dve.wait_ge(work_free, at + 1)
                dve.tensor_scalar(cols[n][:, 1::2, :], cols[n][:, 1::2, :], 1.0, None, ALU.add).then_inc(mod_step, 1)
                at = work.next()
                dve.wait_ge(work_full, at + 1)
                g = gates[n][:, :, :]
                dve.tensor_copy(g, bank[at % WORK][:, 0:2 * D].rearrange("p (a d) -> p a d", a=2)).then_inc(work_free, 1)
                dve.wait_ge(work_free, at + 1)
                dve.tensor_scalar(gsgn[:, :, :], g, 0.0, 2.0, ALU.is_ge, ALU.mult).then_inc(mod_step, 1)
                dve.scalar_tensor_tensor(gabs[:, :, :], g, -1.0, g, ALU.mult, ALU.max).then_inc(mod_step, 1)
                dve.wait_ge(mod_step, 5 * n + 3)
                dve.tensor_scalar(gabs[:, :, :], gabs[:, :, :], LEAST_GATE, None, ALU.max).then_inc(mod_step, 1)
                dve.wait_ge(mod_step, 5 * n + 4)
                dve.scalar_tensor_tensor(g, gsgn[:, :, :], -1.0, gabs[:, :, :], ALU.add, ALU.mult).then_inc(mod_step, 1)

            def norm(n):
                xh, hfb = mo(n)
                layer, v = n // 2, 2 * (n % 2)
                if n:
                    dve.wait_ge(x_done[n - 1], XD[n - 1])
                for t in range(NT):
                    if n == 0 and t % TC == 0:
                        dve.wait_ge(x_loaded[t // TC], 16)
                    dve.bn_stats(stats[:, t, :], x[:, t, :]).then_inc(n_step[n], 1)
                dve.wait_ge(n_step[n], NT)
                dve.tensor_tensor(msum[:, :], stats[:, :, 1], stats[:, :, 4], ALU.add).then_inc(n_step[n], 1)
                dve.tensor_tensor(mdif[:, :], stats[:, :, 1], stats[:, :, 4], ALU.subtract).then_inc(n_step[n], 1)
                dve.tensor_tensor(vsum[:, :], stats[:, :, 2], stats[:, :, 5], ALU.add).then_inc(n_step[n], 1)
                dve.wait_ge(n_step[n], NT + 3)
                dve.tensor_tensor(mdif[:, :], mdif[:, :], mdif[:, :], ALU.mult).then_inc(n_step[n], 1)
                dve.tensor_scalar(msum[:, :], msum[:, :], 0.5, None, ALU.mult).then_inc(n_step[n], 1)
                dve.wait_ge(n_step[n], NT + 4)
                dve.scalar_tensor_tensor(vsum[:, :], mdif[:, :], D / 4, vsum[:, :], ALU.mult, ALU.add).then_inc(n_step[n], 1)
                dve.wait_ge(n_std[n], 1)
                dve.reciprocal(rstd[:, :], rstd[:, :]).then_inc(n_step[n], 1)
                dve.wait_ge(n_step[n], NT + 7)
                first = work.at()
                lo_of = lambda u: (h_lo[:, u % KB, u // KB * CH:(u // KB + 1) * CH], h_hi[:, u % KB, u // KB * CH:(u // KB + 1) * CH])

                def lo_part(u):
                    lo, hi = lo_of(u)
                    dve.wait_ge(n_hi[n], u + 1)
                    dve.tensor_tensor(lo, hfb[:, u % 4, :], hi.bitcast(F32), ALU.subtract).then_inc(n_lo[n], 1)

                def turned(c):
                    for k in range(KB):
                        u, at = c * KB + k, work.next()
                        dve.wait_ge(work_full, at + 1)
                        dve.tensor_scalar(hfb[:, u % 4, :], bank[at % WORK][:, :], cols[layer][:, v + 1, k:k + 1],
                                          cols[layer][:, v, k:k + 1], ALU.mult, ALU.add).then_inc(work_free, 1)
                        if u >= 1:
                            lo_part(u - 1)

                for c in range(NC_):
                    if c >= 2:
                        dve.wait_ge(work_full, first + KB * (c - 1))
                    for t in range(c * TC, (c + 1) * TC):
                        dve.tensor_scalar(xh[:, t % (2 * TC), :], x[:, t, :], msum[:, t:t + 1], rstd[:, t:t + 1],
                                          ALU.subtract, ALU.mult).then_inc(n_xhat[n], 1)
                    if c >= 1:
                        turned(c - 1)
                turned(NC_ - 1)
                lo_part(NC_ * KB - 1)

            def tables():
                dve.wait_ge(consts, 8)
                dve.tensor_copy(lag[:, :], lag_i[:, :]).then_inc(a_tab, 1)
                dve.tensor_copy(rowf[:, :], rowi[:, :]).then_inc(a_tab, 1)
                dve.tensor_copy(endf[:, :], endi[:, :]).then_inc(a_tab, 1)
                dve.wait_ge(a_loaded[3], 16)
                dve.tensor_scalar(nslope[:, :], nslope[:, :], -1.0, None, ALU.mult).then_inc(a_tab, 1)
                dve.wait_ge(a_loaded[4], 16 * HG)
                dve.tensor_scalar(nslope_s[:, :], nslope_s[:, :], -1.0, None, ALU.mult).then_inc(a_tab, 1)
                dve.wait_ge(a_tab, 5)
                dve.tensor_scalar(lag[:, :], lag[:, :], 0.0, None, ALU.max).then_inc(a_tab, 1)

            def linear_attention():
                dve.wait_ge(a_exp, A_EXPS)
                dve.wait_ge(a_sel, 2)
                dve.memset(kv[:, :, :], 0.0).then_inc(a_kv, G0)
                with dve.Fori(0, NC_) as i:
                    work.enter(i, A_WORK)
                    token = lambda t: i * TC + t

                    for g in range(G0):
                        work.next()
                        work.next()
                        dve.wait_ge(a_silu, i * 2 * G0 + 2 * g + 2)
                        dve.tensor_tensor(qdT[:, g, :].rearrange("p (t m) -> p t m", m=P), qT[:, g, :].rearrange("p (t m) -> p t m", m=P),
                                          qdec[:, g:g + 1, :].to_broadcast([P, TC, P]), ALU.mult).then_inc(work_free, 2)

                    def by_token(t):
                        at = work.next()
                        dve.wait_ge(a_ks, token(t) + 1)
                        dve.tensor_tensor(kd[:, t % 2, :, 0:D0], ksil[:, t % 2, :].rearrange("p (h d) -> p h d", d=D0),
                                          kdec[:, :].rearrange("p (h a) -> p h a", a=1).to_broadcast([P, H0, D0]), ALU.mult).then_inc(a_kd, 1)
                        dve.tensor_copy(vt[:, t % 2, :], bank[(work.fixed - 1) % WORK][:, D:2 * D]).then_inc(work_free, 1)
                        work.next()
                        dve.wait_ge(work_full, at + 2)
                        dve.tensor_copy(ut[:, t % 2, :], bank[(work.fixed - 1) % WORK][:, 0:D]).then_inc(work_free, 1)

                    def out_lo(t):
                        at = work.next()
                        dve.wait_ge(a_ohi, token(t) + 1)
                        dve.tensor_tensor(oT_lo[:, t, :], bank[(work.fixed - 1) % WORK][:, 0:D], oT_hi[:, t, :].bitcast(F32),
                                          ALU.subtract).then_inc(work_free, 1)

                    by_token(0)
                    for t in range(TC):
                        for r in range(HG):
                            dve.wait_ge(a_score, token(t) * HG + r + 1)
                            dve.tensor_tensor(amat[:, r, :, :], bank[SIDE + r][:, :].rearrange("p (g m) -> p g m", m=P),
                                              decay[:, r, :, :], ALU.mult).then_inc(a_mask, 1)
                        if t < TC - 1:
                            by_token(t + 1)
                        if t >= 1:
                            out_lo(t - 1)
                        at = work.next()
                        dve.wait_ge(a_sq, token(t) + 1)
                        dve.tensor_tensor(ou[:, t % 2, :], bank[(work.fixed - 1) % WORK][:, 0:D], ut[:, t % 2, :],
                                          ALU.mult).then_inc(work_free, 1)
                        at = work.next()
                        dve.wait_ge(work_full, at + 1)
                        dve.tensor_tensor(kvn[:, :, :].rearrange("p g (r d) -> p g r d", d=D0),
                                          bank[(work.fixed - 1) % WORK][:, 0:D].rearrange("p (g r d) -> p g r d", r=HG, d=D0),
                                          own[:, :, :].rearrange("p (a r) d -> p a r d", a=1).to_broadcast([P, G0, HG, D0]),
                                          ALU.mult).then_inc(work_free, 1)
                        dve.wait_ge(work_free, at + 1)
                        dve.wait_ge(a_kv, token(t) * G0 + G0)
                        for g in range(G0):
                            dve.scalar_tensor_tensor(kv[:, g, :], kv[:, g, :], bdec[:, g:g + 1], kvn[:, g, :],
                                                     ALU.mult, ALU.add).then_inc(a_kv, 1)
                    out_lo(TC - 1)
                    dve.wait_ge(a_std, i + 1)
                    dve.reciprocal(rms[:, :], rms[:, :]).then_inc(a_rms, 1)
                    dve.wait_ge(a_rms, i + 1)
                    for t in range(TC):
                        at = work.next()
                        dve.wait_ge(work_full, at + 1)
                        xt = x[:, bass.ds(i * TC + t, 1), :].rearrange("p a d -> p (a d)")
                        dve.scalar_tensor_tensor(xt, bank[(work.fixed - 1) % WORK][:, 0:D], rms[:, t:t + 1], xt,
                                                 ALU.mult, ALU.add).then_inc(work_free, 1)
                work.leave(NC_)
                dve.wait_ge(work_free, work.at())
                dve.tensor_copy(rms[:, 0:1], ssq[:, 0:1]).then_inc(x_done[0], XD[0])

            def mixture(n):
                F, tiles, T = F_L[n], m_tiles[n], m_count[n]
                dve.wait_ge(m_rt[n], 16)
                step = [0]

                def done(ins):
                    step[0] += 1
                    ins.then_inc(m_top[n], 1)
                    dve.wait_ge(m_top[n], step[0])

                done(dve.tensor_copy(rt_hi[:, :, :], rt[:, :, :]))
                done(dve.tensor_tensor(rt_lo[:, :, :], rt[:, :, :], rt_hi[:, :, :].bitcast(F32), ALU.subtract))
                dve.wait_ge(m_sc[n], 1)
                done(dve.tensor_copy(sc[:, :, :].rearrange("p t e -> p (t e)"), bank[SIDE][:, 0:NT * E]))
                done(dve.tensor_reduce(top[:, :], sc[:, :, :], AX.X, ALU.max))
                row = sc[:, :, :].rearrange("p t (a e) -> p t a e", a=1).to_broadcast([P, NT, E, E])
                col = sc[:, :, :].rearrange("p t (e a) -> p t e a", a=1).to_broadcast([P, NT, E, E])
                done(dve.tensor_tensor(gt, row, col, ALU.is_gt))
                done(dve.tensor_tensor(eq, row, col, ALU.is_equal))
                dve.wait_ge(m_zero, 5 * n + 5)
                done(dve.tensor_tensor(eq, eq, low[:, :, :].rearrange("p (a e) f -> p a e f", a=1).to_broadcast([P, NT, E, E]), ALU.mult))
                done(dve.tensor_tensor(gt, gt, eq, ALU.add))
                done(dve.tensor_reduce(rank[:, :, :], gt, AX.X, ALU.add))
                done(dve.tensor_tensor(sc[:, :, :], sc[:, :, :], top[:, :].rearrange("p (t a) -> p t a", a=1).to_broadcast([P, NT, E]),
                                       ALU.subtract))
                dve.wait_ge(m_exp[n], 1)
                done(dve.scalar_tensor_tensor(comb[:, :, 0:E], rank[:, :, :], 2.0, sc[:, :, :], ALU.is_lt, ALU.mult))
                done(dve.tensor_reduce(den[:, :], comb[:, :, 0:E], AX.X, ALU.add))
                done(dve.reciprocal(den[:, :], den[:, :]))
                done(dve.tensor_tensor(comb[:, :, 0:E], comb[:, :, 0:E],
                                       den[:, :].rearrange("p (t a) -> p t a", a=1).to_broadcast([P, NT, E]), ALU.mult))
                done(dve.memset(comb[:, :, E:E + 1], 1.0))
                dve.memset(spare[:, :], 0.0).then_inc(x_done[2 * n + 1], 1)

                tile, y, added = Turn(), Turn(), Turn()
                nf = len(tiles)

                def expert(e, half):
                    for c in range(NC_):
                        def lo_part():
                            u = lo.next()
                            w = tiles[f_of[0]][1]
                            f_of[0] += 1
                            dve.wait_ge(m_hi[n], u + 1)
                            s = (lo.fixed - 1) % HID
                            dve.tensor_tensor(hid_lo[0:w, s, :], hid[0:w, (lo.fixed - 1) % 2, :], hid_hi[0:w, s, :].bitcast(F32),
                                              ALU.subtract).then_inc(m_lo[n], 1)

                        f_of = [0]
                        lo.fixed = tile.fixed
                        for f, (f0, w) in enumerate(tiles):
                            u = tile.next()
                            at = work.next()
                            work.next()
                            dve.wait_ge(m_sil[n], u + 1)
                            dve.wait_ge(work_full, at + 2)
                            if f == 0:
                                dve.wait_ge(x_done[2 * n + 1], added.at() + 1)
                            elif f > 1:
                                dve.wait_ge(m_lo[n], u - 1)
                            dve.tensor_tensor(hid[0:w, (tile.fixed - 1) % 2, :], bank[(work.fixed - 1) % WORK][0:w, :],
                                              sil[0:w, (tile.fixed - 1) % 2, :], ALU.mult).then_inc(work_free, 2)
                            if f:
                                lo_part()
                        lo_part()
                        dve.wait_ge(x_done[2 * n + 1], added.at() + 1)
                        for t in range(TC):
                            if t % 2 == 0:
                                yu = y.next()
                                dve.wait_ge(m_y[n], yu + 1)
                            added.next()
                            k = c * TC + t
                            dve.scalar_tensor_tensor(x[:, k, :], bank[SIDE + (y.fixed - 1) % 4][:, t % 2 * D:(t % 2 + 1) * D],
                                                     comb[:, k, bass.ds(e, 1)], x[:, k, :], ALU.mult, ALU.add).then_inc(x_done[2 * n + 1], 1)

                lo = Turn()
                rounds = (T - 1) // 2
                with dve.Fori(0, rounds) as i:
                    for turn, per in ((work, 2 * nf * NC_), (tile, nf * NC_), (lo, nf * NC_), (y, 2 * NC_), (added, NT)):
                        turn.enter(i, 2 * per)
                    for half in range(2):
                        expert(2 * i + half, half)
                for turn in (work, tile, lo, y, added):
                    turn.leave(rounds)
                for e in range(2 * rounds, T):
                    expert(e, e % 2)

            def softmax_attention():
                work_s, pt, added = Turn(), Turn(), Turn()
                rows = Turn()
                z = Turn()
                his = Turn()
                exps = Turn()
                dve.memset(rinv[:, :, :], 0.0).then_inc(s_free, S_RING)
                dve.memset(spare[:, :], 0.0).then_inc(x_done[2], 1)
                dve.wait_ge(s_neg, 2)

                def projected(lo, hi, scale=None):
                    u, b = work_s.next(), bank[(work_s.fixed - 1) % S_RING]
                    dve.wait_ge(s_hi, his.next() + 1)
                    src = b[:, :]
                    if len(lo.shape) == 3:
                        src = src.rearrange("p (t h) -> p t h", t=2)
                    if scale is None:
                        dve.tensor_tensor(lo, src, hi.bitcast(F32), ALU.subtract).then_inc(s_free, 1)
                    else:
                        dve.scalar_tensor_tensor(lo, src, scale, hi.bitcast(F32), ALU.mult, ALU.subtract).then_inc(s_free, 1)

                def keys(j, q):
                    for c in range(NC_):
                        projected(KT_lo[:, c * CH:(c + 1) * CH], KT_hi[:, c * CH:(c + 1) * CH])

                def queries(j, q):
                    projected(QT_lo[:, q % 2, :], QT_hi[:, q % 2, :], DH ** -0.5)

                def values(j, q):
                    for t in range(0, NT, 2):
                        projected(V_lo[:, t:t + 2, :], V_hi[:, t:t + 2, :])

                def scores(j, q):
                    p = prob[q % 2]
                    for r in range(TC):
                        at0, width = row_start(q, r), row_width(q, r)
                        for c in range(q + 1):
                            u, b = work_s.next(), bank[(work_s.fixed - 1) % S_RING]
                            dve.wait_ge(s_full, u + 1)
                            n = CH if c < q else r * P
                            if n:
                                ins = dve.tensor_scalar(p[:, at0 + c * CH:at0 + c * CH + n], b[:, 0:n], 1.0, LOWEST, ALU.mult, ALU.max,
                                                        accum_out=p[:, at0 + width + c:at0 + width + c + 1])
                            if c < q:
                                ins.then_inc(s_free, 1)
                            else:
                                dve.tensor_tensor(p[:, at0 + width - P:at0 + width], b[:, n:n + P], negmask[:, :], ALU.add).then_inc(s_free, 1)
                        dve.wait_ge(s_free, u + 1 + S_RING)
                        rows.next()
                        dve.tensor_reduce(nmax[:, q, r:r + 1], p[:, at0 + width - P:at0 + width + q + (r > 0)], AX.X, ALU.max,
                                          negate=True).then_inc(s_row, 1)

                def turned(j, q):
                    for kt in range(TC * (q + 1)):
                        r0 = max(0, kt - TC * q) * P
                        u = pt.next()
                        s = (pt.fixed - 1) % 4
                        dve.wait_ge(s_phi, u + 1)
                        dve.tensor_tensor(pT_lo[:, s, r0:CH], bank[S_RING + s][:, r0:CH], pT_hi[:, s, r0:CH].bitcast(F32),
                                          ALU.subtract).then_inc(s_plo, 1)
                    dve.wait_ge(s_zhi, z.next() + 1)
                    dve.tensor_tensor(zT_lo[:, :], bank[Z_BANK][:, :], zT_hi[:, :].bitcast(F32), ALU.subtract).then_inc(s_zlo, 1)

                def outputs(j, q):
                    e = exps.next()
                    dve.wait_ge(s_exp, ROWS_BY[j, q] + rounds_rows())
                    dve.reciprocal(rinv[:, q, :], rsum[:, q, :]).then_inc(s_inv, 1)
                    dve.wait_ge(s_inv, e + 1)
                    dve.wait_ge(x_done[2], added.at() + 1)
                    for t in range(TC):
                        if t % 2 == 0:
                            u = work_s.next()
                            dve.wait_ge(s_full, u + 1)
                            b = bank[(work_s.fixed - 1) % S_RING]
                        k = q * TC + t
                        ins = dve.scalar_tensor_tensor(x[:, k, :], b[:, t % 2 * D:(t % 2 + 1) * D], rinv[:, q, t:t + 1], x[:, k, :],
                                                       ALU.mult, ALU.add)
                        added.next()
                        ins.then_inc(x_done[2], 1)
                        if t % 2:
                            dve.wait_ge(x_done[2], added.at() + 1)
                            dve.memset(spare[:, :], 0.0).then_inc(s_free, 1)

                steps = {"K": keys, "Q": queries, "V": values, "S": scores, "T": turned, "O": outputs}
                with dve.Fori(0, H1 // 2) as i:
                    rounds_rows = lambda: i * (2 * NT)
                    work_s.enter(i, PAIR_WORK)
                    for turn, per in ((pt, 2 * HEAD_PT), (added, 2 * NT), (rows, 2 * NT), (z, 2 * NC_),
                                      (his, NT // 2 + 4 * NC_), (exps, 2 * NC_)):
                        turn.enter(i, per)
                    for what, j, q in ORDER:
                        steps[what](j, q)
                for turn in (work_s, pt, added, rows, z, his, exps):
                    turn.leave(H1 // 2)

            tables()
            norm(0)
            linear_attention()
            if stop >= 1:
                norm(1)
                mixture(0)
            if stop >= 2:
                norm(2)
                softmax_attention()
            if stop >= 3:
                norm(3)
                mixture(1)

        @block.scalar
        def _(act):
            work = Turn()
            for n in range(2):
                act.wait_ge(c_loaded, 16 * (n + 1))
                if n:
                    act.wait_ge(c_wide, KB)
                act.activation(csil[:, :], cin[:, :], ACT.Silu).then_inc(c_silu, 1)
                work.fixed += 2

            def norm(n):
                _, hfb = mo(n)
                act.wait_ge(n_step[n], NT + 6)
                act.activation(rstd[:, :], vsum[:, :], ACT.Sqrt, scale=1.0 / D, bias=eps_ln[:, :]).then_inc(n_std[n], 1)
                for u in range(NC_ * KB):
                    at = work.next()
                    act.wait_ge(work_free, at + 1)
                    act.activation(h_hi[:, u % KB, u // KB * CH:(u // KB + 1) * CH], hfb[:, u % 4, :], ACT.Copy).then_inc(n_hi[n], 1)

            def tables():
                act.wait_ge(a_tab, 6)
                for g in range(G0):
                    for r in range(HG):
                        h = g * HG + r
                        act.activation(decay[:, r, g, :], lag[:, :], ACT.Exp, scale=nslope[:, h:h + 1]).then_inc(a_exp, 1)
                for g in range(G0):
                    act.activation(qdec[:, g, :], rowf[:, :], ACT.Exp, scale=nslope_s[:, g:g + 1]).then_inc(a_exp, 1)
                act.activation(kdec[:, :], nslope[:, :], ACT.Exp, scale=endf[:, :]).then_inc(a_exp, 1)
                act.activation(bdec[:, :], nslope_s[:, :], ACT.Exp, scale=float(P)).then_inc(a_exp, 1)

            def linear_attention():
                with act.Fori(0, NC_) as i:
                    work.enter(i, A_WORK)
                    token = lambda t: i * TC + t
                    for g in range(G0):
                        for dst in (qT, kT):
                            at = work.next()
                            act.wait_ge(work_full, at + 1)
                            act.activation(dst[:, g, :], bank[(work.fixed - 1) % WORK][:, :], ACT.Silu).then_inc(a_silu, 1)

                    def by_token(t):
                        at = work.next()
                        act.wait_ge(work_full, at + 1)
                        act.activation(ksil[:, t % 2, :], bank[(work.fixed - 1) % WORK][:, 0:D], ACT.Silu).then_inc(a_ks, 1)
                        work.next()

                    def out_hi(t):
                        at = work.next()
                        act.wait_ge(work_full, at + 1)
                        act.activation(oT_hi[:, t, :], bank[(work.fixed - 1) % WORK][:, 0:D], ACT.Copy).then_inc(a_ohi, 1)

                    by_token(0)
                    for t in range(TC):
                        if t < TC - 1:
                            by_token(t + 1)
                        if t >= 1:
                            out_hi(t - 1)
                        at = work.next()
                        act.wait_ge(work_full, at + 1)
                        act.activation(osq[:, :], bank[(work.fixed - 1) % WORK][:, 0:D], ACT.Square,
                                       accum_out=ssq[:, t:t + 1]).then_inc(a_sq, 1)
                        work.next()
                    out_hi(TC - 1)
                    act.wait_ge(a_sq, i * TC + TC)
                    act.activation(rms[:, :], ssq[:, :], ACT.Sqrt, scale=1.0 / D, bias=eps_rms[:, :]).then_inc(a_std, 1)
                    work.fixed += TC
                work.leave(NC_)

            def mixture(n):
                tiles, T = m_tiles[n], m_count[n]
                nf = len(tiles)
                act.wait_ge(m_top[n], 10)
                act.activation(sc[:, :, :], sc[:, :, :], ACT.Exp).then_inc(m_exp[n], 1)
                tile, hi = Turn(), Turn()

                def expert():
                    for c in range(NC_):
                        def hi_part(f, at):
                            w = tiles[f][1]
                            hi.next()
                            act.wait_ge(work_free, at + 2)
                            act.activation(hid_hi[0:w, (hi.fixed - 1) % HID, :], hid[0:w, (hi.fixed - 1) % 2, :],
                                           ACT.Copy).then_inc(m_hi[n], 1)

                        before = None
                        for f, (f0, w) in enumerate(tiles):
                            tile.next()
                            at = work.next()
                            work.next()
                            act.wait_ge(work_full, at + 1)
                            act.wait_ge(work_free, at - 2)
                            act.activation(sil[0:w, (tile.fixed - 1) % 2, :], bank[(work.fixed - 2) % WORK][0:w, :],
                                           ACT.Silu).then_inc(m_sil[n], 1)
                            if f:
                                hi_part(f - 1, before)
                            before = at
                        hi_part(nf - 1, before)

                rounds = (T - 1) // 2
                with act.Fori(0, rounds) as i:
                    for turn, per in ((work, 2 * nf * NC_), (tile, nf * NC_), (hi, nf * NC_)):
                        turn.enter(i, 2 * per)
                    for half in range(2):
                        expert()
                for turn in (work, tile, hi):
                    turn.leave(rounds)
                for e in range(2 * rounds, T):
                    expert()

            def softmax_attention():
                work_s, pt, z, rows = Turn(), Turn(), Turn(), Turn()

                def projected(hi, scale=1.0):
                    u, b = work_s.next(), bank[(work_s.fixed - 1) % S_RING]
                    src = b[:, :]
                    if len(hi.shape) == 3:
                        src = src.rearrange("p (t h) -> p t h", t=2)
                    act.wait_ge(s_full, u + 1)
                    act.activation(hi, src, ACT.Copy, scale=scale).then_inc(s_hi, 1)

                def keys(j, q):
                    for c in range(NC_):
                        projected(KT_hi[:, c * CH:(c + 1) * CH])

                def queries(j, q):
                    projected(QT_hi[:, q % 2, :], DH ** -0.5)

                def values(j, q):
                    for t in range(0, NT, 2):
                        projected(V_hi[:, t:t + 2, :])

                def scores(j, q):
                    for r in range(TC):
                        at0, width = row_start(q, r), row_width(q, r)
                        work_s.fixed += q + 1
                        act.wait_ge(s_row, rows.next() + 1)
                        act.activation(prob[q % 2][:, at0:at0 + width], prob[q % 2][:, at0:at0 + width], ACT.Exp,
                                       bias=nmax[:, q, r:r + 1], accum_out=rsum[:, q, r:r + 1]).then_inc(s_exp, 1)

                def turned(j, q):
                    for kt in range(TC * (q + 1)):
                        r0 = max(0, kt - TC * q) * P
                        u = pt.next()
                        s = (pt.fixed - 1) % 4
                        act.wait_ge(s_pt, u + 1)
                        act.activation(pT_hi[:, s, r0:CH], bank[S_RING + s][:, r0:CH], ACT.Copy).then_inc(s_phi, 1)
                    act.wait_ge(s_z, z.next() + 1)
                    act.activation(zT_hi[:, :], bank[Z_BANK][:, :], ACT.Copy).then_inc(s_zhi, 1)

                def outputs(j, q):
                    work_s.fixed += TC // 2

                steps = {"K": keys, "Q": queries, "V": values, "S": scores, "T": turned, "O": outputs}
                with act.Fori(0, H1 // 2) as i:
                    for turn, per in ((work_s, PAIR_WORK), (pt, 2 * HEAD_PT), (z, 2 * NC_), (rows, 2 * NT)):
                        turn.enter(i, per)
                    for what, j, q in ORDER:
                        steps[what](j, q)
                for turn in (work_s, pt, z, rows):
                    turn.leave(H1 // 2)

            tables()
            norm(0)
            linear_attention()
            if stop >= 1:
                norm(1)
                mixture(0)
            if stop >= 2:
                norm(2)
                softmax_attention()
            if stop >= 3:
                norm(3)
                mixture(1)

        @block.tensor
        def _(pe):
            work = Turn()

            def work_bank():
                at = work.next()
                wait(pe, work_free, at + 1 - WORK)
                return bank[(work.fixed - 1) % WORK]

            def three(dst, lhs, rhs, first, last):
                for a, b in ((0, 0), (0, 1), (1, 0)):
                    ins = pe.matmul(dst, lhs[a], rhs[b], start=first and (a, b) == (0, 0),
                                    stop=last and (a, b) == (1, 0), skip_group_check=True)
                return ins

            for n in range(2):
                pe.wait_ge(wmod_loaded, 16 * (n + 1))
                pe.wait_ge(c_silu, n + 1)
                b = work_bank()
                for v, part in enumerate((0, 1, 3, 4)):
                    for k in range(KB):
                        for kk in range(KB):
                            ins = pe.matmul(b[:, v * KB + k:v * KB + k + 1],
                                            wmod[:, kk, part * D + k * P:part * D + (k + 1) * P], csil[:, kk:kk + 1],
                                            start=v + k + kk == 0, stop=kk == KB - 1, skip_group_check=True)
                ins.then_inc(work_full, 1)
                pe.wait_ge(c_wide, KB * (n + 1))
                b = work_bank()
                for g, part in enumerate((2, 5)):
                    for kk in range(KB):
                        ins = pe.matmul(b[:, g * D:(g + 1) * D], cwide[:, kk, :], wmod[:, kk, part * D:(part + 1) * D],
                                        start=g + kk == 0, stop=kk == KB - 1, skip_group_check=True)
                ins.then_inc(work_full, 1)

            def norm(n):
                xh, _ = mo(n)
                for c in range(NC_):
                    pe.wait_ge(n_xhat[n], (c + 1) * TC)
                    for k in range(KB):
                        b = work_bank()
                        for t in range(TC):
                            ins = pe.transpose(b[:, t * P:(t + 1) * P], xh[:, (c * TC + t) % (2 * TC), k * P:(k + 1) * P], ident[:, :])
                        ins.then_inc(work_full, 1)

            def linear_attention():
                pe.wait_ge(a_split, 13)
                pe.wait_ge(a_sel, 2)
                with pe.Fori(0, NC_) as i:
                    work.enter(i, A_WORK)
                    token = lambda t: i * TC + t
                    hc = (hc_hi, hc_lo)
                    pe.wait_ge(a_hc, i * 2 * KB + 2 * KB)
                    for g in range(G0):
                        for m in (g, G0 + g):
                            b = work_bank()
                            for k in range(KB):
                                ins = three(b[:, :], [w[:, k, m, :] for w in (wqk_hi, wqk_lo)], [h[:, k, :] for h in hc],
                                            k == 0, k == KB - 1)
                            ins.then_inc(work_full, 1)
                    features = work.at()

                    def by_token(t):
                        for c0_, c1_ in ((0, 2 * D), (2 * D, 3 * D)):
                            b = work_bank()
                            for k in range(KB):
                                ins = three(b[:, 0:c1_ - c0_], [h[:, k, t * P:(t + 1) * P] for h in hc],
                                            [w[:, k, c0_:c1_] for w in (wkvu_hi, wkvu_lo)], k == 0, k == KB - 1)
                            ins.then_inc(work_full, 1)
                        return work.at()

                    def turn_out(t, gated):
                        b = work_bank()
                        pe.wait_ge(work_free, gated + 1)
                        for k in range(KB):
                            ins = pe.transpose(b[:, k * P:(k + 1) * P], ou[:, t % 2, k * P:(k + 1) * P], ident[:, :])
                        ins.then_inc(work_full, 1)
                        return work.at()

                    by = by_token(0)
                    gated = lo_done = None
                    for t in range(TC):
                        cut = slice(t * P, (t + 1) * P)
                        pe.wait_ge(work_free, features)
                        for r in range(HG):
                            for g in range(G0):
                                s = slice(r * STRIP, r * STRIP + D0)
                                ins = pe.matmul(bank[SIDE + r][:, g * P:(g + 1) * P], kT[s, g, cut], qT[s, g, cut],
                                                start=g == 0, stop=True, skip_group_check=True)
                            ins.then_inc(a_score, 1)
                        nxt = by_token(t + 1) if t < TC - 1 else None
                        if t >= 1:
                            turn_out(t - 1, gated)
                        b = work_bank()
                        gated = work.at() - 1
                        pe.wait_ge(a_kv, token(t) * G0 + G0)
                        for g in range(G0):
                            pe.matmul(b[:, g * HG * D0:(g + 1) * HG * D0], qdT[:, g, cut], kv[:, g, :],
                                      start=g == 0, stop=False, skip_group_check=True)
                        pe.wait_ge(work_free, by)
                        pe.wait_ge(a_mask, token(t) * HG + HG)
                        for g in range(G0):
                            for r in range(HG):
                                h = g * HG + r
                                ins = pe.matmul(b[:, h * D0:(h + 1) * D0], amat[:, r, g, :], vt[:, t % 2, h * D0:(h + 1) * D0],
                                                start=False, stop=True, skip_group_check=True)
                        ins.then_inc(work_full, 1)
                        b = work_bank()
                        pe.wait_ge(a_kd, token(t) + 1)
                        for g in range(G0):
                            ins = pe.matmul(b[:, g * HG * D0:(g + 1) * HG * D0], kd[:, t % 2, g * HG:(g + 1) * HG, :].rearrange("p r s -> p (r s)"),
                                            vt[:, t % 2, g * HG * D0:(g + 1) * HG * D0], start=g == 0, stop=True, skip_group_check=True)
                        ins.then_inc(work_full, 1)
                        by = nxt
                    split_at = turn_out(TC - 1, gated)
                    for t in range(TC):
                        b = work_bank()
                        if t == 0:
                            pe.wait_ge(work_free, split_at)
                        for k in range(KB):
                            ins = three(b[:, 0:D], [o[:, t, k * P:(k + 1) * P] for o in (oT_hi, oT_lo)],
                                        [w[:, k, :] for w in (wo0_hi, wo0_lo)], k == 0, k == KB - 1)
                        ins.then_inc(work_full, 1)
                work.leave(NC_)

            def mixture(n):
                F, tiles, T = F_L[n], m_tiles[n], m_count[n]
                nf = len(tiles)
                h = (h_hi, h_lo)
                pe.wait_ge(m_top[n], 2)
                pe.wait_ge(n_lo[2 * n + 1], NC_ * KB)
                for t in range(NT):
                    for k in range(KB):
                        ins = three(bank[SIDE][:, t * E:(t + 1) * E], [a[:, k, t * P:(t + 1) * P] for a in h],
                                    [r[:, k, :] for r in (rt_hi, rt_lo)], t == 0 and k == 0, k == KB - 1)
                ins.then_inc(m_sc[n], 1)
                tile, y = Turn(), Turn()

                def expert(e, half):
                    gu, dn = (gu_hi[half], gu_lo[half]), (dn_hi[half], dn_lo[half])
                    pe.wait_ge(m_raw[n], e * 5 + 2)
                    for c in range(NC_):
                        first = tile.fixed
                        for f0, w in tiles:
                            tile.next()
                            for at in (f0, F + f0):
                                b = work_bank()
                                for k in range(KB):
                                    ins = three(b[0:w, :], [a[:, k, at:at + w] for a in gu],
                                                [a[:, k, c * CH:(c + 1) * CH] for a in h], k == 0, k == KB - 1)
                                ins.then_inc(work_full, 1)
                        if c == 0:
                            pe.wait_ge(m_raw[n], e * 5 + 5)
                        banks = []
                        for _ in range(2):
                            y.next()
                            banks.append(bank[SIDE + (y.fixed - 1) % 4])
                        if n == 0 or n == 1:
                            pe.wait_ge(m_top[n], 3)
                        for f in range(nf):
                            s = (first + f) % HID
                            pe.wait_ge(m_lo[n], tile.at() - nf + f + 1)
                            for t in range(TC):
                                ins = three(banks[t // 2][:, t % 2 * D:(t % 2 + 1) * D],
                                            [a[:, s, t * P:(t + 1) * P] for a in (hid_hi, hid_lo)],
                                            [a[:, f, :] for a in dn], f == 0 and t % 2 == 0, f == nf - 1)
                                if f == nf - 1 and t % 2:
                                    ins.then_inc(m_y[n], 1)

                rounds = (T - 1) // 2
                with pe.Fori(0, rounds) as i:
                    for turn, per in ((work, 2 * nf * NC_), (tile, nf * NC_), (y, 2 * NC_)):
                        turn.enter(i, 2 * per)
                    for half in range(2):
                        expert(2 * i + half, half)
                for turn in (work, tile, y):
                    turn.leave(rounds)
                for e in range(2 * rounds, T):
                    expert(e, e % 2)

            def softmax_attention():
                work_s, pt, z, rows = Turn(), Turn(), Turn(), Turn()
                h = (h_hi, h_lo)
                pe.wait_ge(n_lo[2], NC_ * KB)
                key_at, query_at, value_at, rows_at, z_at = {}, {}, {}, {}, {}

                def ring():
                    at = work_s.next()
                    pe.wait_ge(s_free, at + 1)
                    return bank[(work_s.fixed - 1) % S_RING]

                def read(at):
                    pe.wait_ge(s_free, at + 1 + S_RING)

                def keys(j, q):
                    pe.wait_ge(s_split, rounds_of(PAIR_SPLIT) + 4 + 2 * j)
                    for c in range(NC_):
                        b = ring()
                        for k in range(KB):
                            ins = three(b[:, :], [w[:, k, 2 * j * DH:(2 * j + 1) * DH] for w in (wkq_hi, wkq_lo)],
                                        [a[:, k, c * CH:(c + 1) * CH] for a in h], k == 0, k == KB - 1)
                        ins.then_inc(s_full, 1)

                def queries(j, q):
                    b = ring()
                    query_at[j, q] = work_s.at() - 1
                    for k in range(KB):
                        ins = three(b[:, :], [w[:, k, (2 * j + 1) * DH:(2 * j + 2) * DH] for w in (wkq_hi, wkq_lo)],
                                    [a[:, k, q * CH:(q + 1) * CH] for a in h], k == 0, k == KB - 1)
                    ins.then_inc(s_full, 1)

                def values(j, q):
                    pe.wait_ge(s_split, rounds_of(PAIR_SPLIT) + 2)
                    for t in range(NT):
                        if t % 2 == 0:
                            b = ring()
                        for k in range(KB):
                            ins = three(b[:, t % 2 * 2 * DH:(t % 2 + 1) * 2 * DH], [a[:, k, t * P:(t + 1) * P] for a in h],
                                        [w[:, k, :] for w in (wv_hi, wv_lo)], t % 2 == 0 and k == 0, k == KB - 1)
                        if t % 2:
                            ins.then_inc(s_full, 1)
                    value_at[0] = work_s.at() - 1

                def scores(j, q):
                    read(query_at[j, q])
                    for r in range(TC):
                        for c in range(q + 1):
                            b = ring()
                            n = CH if c < q else (r + 1) * P
                            three(b[:, 0:n], [a[:, q % 2, r * P:(r + 1) * P] for a in (QT_hi, QT_lo)],
                                  [a[:, c * CH:c * CH + n] for a in (KT_hi, KT_lo)], True, True).then_inc(s_full, 1)
                        rows.next()
                        rows_at[j, q, r] = rows.at()

                def turn(j, q, kt, s):
                    p = prob[q % 2]
                    for r in range(max(0, kt - TC * q), TC):
                        if kt == 0:
                            pe.wait_ge(s_exp, rows_at[j, q, r])
                        at0 = row_start(q, r) + kt * P
                        ins = pe.transpose(bank[S_RING + s][:, r * P:(r + 1) * P], p[:, at0:at0 + P], ident[:, :])
                    ins.then_inc(s_pt, 1)

                def turned(j, q):
                    count, ahead = TC * (q + 1), 3
                    first = pt.fixed
                    for kt in range(min(ahead, count)):
                        turn(j, q, kt, (first + kt) % 4)
                    if q == 0:
                        read(value_at[0])
                    for kt in range(count):
                        s, r0 = (first + kt) % 4, max(0, kt - TC * q) * P
                        pe.wait_ge(s_plo, pt.next() + 1)
                        ins = three(bank[Z_BANK][:, r0:CH], [a[:, kt, j * DH:(j + 1) * DH] for a in (V_hi, V_lo)],
                                    [a[:, s, r0:CH] for a in (pT_hi, pT_lo)], kt == 0, kt == count - 1)
                        if kt + ahead < count:
                            turn(j, q, kt + ahead, (first + kt + ahead) % 4)
                    ins.then_inc(s_z, 1)
                    z.next()
                    z_at[j, q] = z.at()

                def outputs(j, q):
                    if j == 0 and q == 0:
                        pe.wait_ge(s_split, rounds_of(PAIR_SPLIT) + PAIR_SPLIT)
                    for t in range(TC):
                        if t % 2 == 0:
                            b = ring()
                        if t == 0:
                            pe.wait_ge(s_zlo, z_at[j, q])
                        ins = three(b[:, t % 2 * D:(t % 2 + 1) * D], [a[:, t * P:(t + 1) * P] for a in (zT_hi, zT_lo)],
                                    [w[:, j, :] for w in (wo_hi, wo_lo)], t % 2 == 0, True)
                        if t % 2:
                            ins.then_inc(s_full, 1)

                steps = {"K": keys, "Q": queries, "V": values, "S": scores, "T": turned, "O": outputs}
                with pe.Fori(0, H1 // 2) as i:
                    rounds_of = lambda per: i * per
                    for turn_, per in ((work_s, PAIR_WORK), (pt, 2 * HEAD_PT), (z, 2 * NC_), (rows, 2 * NT)):
                        turn_.enter(i, per)
                    for what, j, q in ORDER:
                        steps[what](j, q)
                for turn_ in (work_s, pt, z, rows):
                    turn_.leave(H1 // 2)

            norm(0)
            linear_attention()
            if stop >= 1:
                norm(1)
                mixture(0)
            if stop >= 2:
                norm(2)
                softmax_attention()
            if stop >= 3:
                norm(3)
                mixture(1)


def arrays_of(inputs):
    import numpy as np

    def a(name):
        return np.asarray(inputs[name])

    d = a("L0_attn_x").shape[-1]
    qkvu = a("L0_attn_W_qkvu").T
    lay = {
        "x": a("L0_attn_x")[0],
        "slope": a("L0_attn_slope_rate"),
        "w_qk": qkvu[:, 0:2 * d],
        "w_kvu": qkvu[:, d:],
        "w_out0": a("L0_attn_W_out").T,
        "router0": a("L0_ffn_w_gate_router").T,
        "gu0": np.concatenate([a("L0_ffn_w_gate_proj"), a("L0_ffn_w_up_proj")], axis=1).transpose(0, 2, 1),
        "down0": a("L0_ffn_w_down_proj").transpose(0, 2, 1),
        "c0": a("L0_c").reshape(-1, 128).T,
        "wmod0": a("L0_wmod"),
        "w_k": a("L1_attn_W_K").transpose(0, 2, 1),
        "w_q": a("L1_attn_W_Q").transpose(0, 2, 1),
        "w_v": a("L1_attn_W_V").transpose(0, 2, 1),
        "w_o": a("L1_attn_W_O").reshape(d, a("L1_attn_W_K").shape[0], -1).transpose(1, 2, 0),
        "router1": a("L1_ffn_gate_w").T,
        "gu1": np.concatenate([a("L1_ffn_expert_gate_up"), a("L1_ffn_base_gate_up")[None]]),
        "down1": np.concatenate([a("L1_ffn_expert_down"), a("L1_ffn_base_down")[None]]),
        "c1": a("L1_c").reshape(-1, 128).T,
        "wmod1": a("L1_wmod"),
    }
    return {k: np.ascontiguousarray(v) for k, v in lay.items()}


def kernel(**inputs):
    import concourse.bacc as bacc
    import numpy as np
    from concourse.bass_utils import run_bass_kernel_spmd

    nc = bacc.Bacc("TRN2", target_bir_lowering=False, num_devices=1)
    arrays, args = {}, []
    for name, a in arrays_of(inputs).items():
        arrays[f"in_{name}_dram"] = a
        args.append(nc.dram_tensor(f"in_{name}_dram", a.shape, mybir.dt.from_np(a.dtype), kind="ExternalInput").ap())
    shape = arrays["in_x_dram"].shape
    args.append(nc.dram_tensor("out_0_dram", shape, F32, kind="ExternalOutput").ap())
    two_blocks(nc, *args)
    r = run_bass_kernel_spmd(nc, [arrays], core_ids=[0])
    return np.asarray(r.results[0]["out_0_dram"]).reshape(1, *shape)
```

```python
from contextlib import ExitStack

import concourse.bass as bass
from concourse import mybir

F32 = mybir.dt.float32
F32R = mybir.dt.float32r
I32 = mybir.dt.int32
ALU = mybir.AluOpType
ACT = mybir.ActivationFunctionType
AX = mybir.AxisListType

P = 128
LN_EPS = 1e-5
RMS_EPS = 1e-6
LEAST_GATE = 0.25
MASKED = -1e10
LOWEST = -3.0e38


class Turn:

    def __init__(self):
        self.fixed, self.round = 0, None

    def at(self):
        return self.fixed if self.round is None else self.fixed + self.round

    def next(self):
        at = self.at()
        self.fixed += 1
        return at

    def enter(self, i, per):
        self.round, self.start, self.per = i * per, self.fixed, per

    def leave(self, rounds):
        assert self.fixed == self.start + self.per, (self.fixed, self.start, self.per)
        self.fixed, self.round = self.start + self.per * rounds, None


def wait(eng, sem, value):
    if isinstance(value, int) and value <= 0:
        return
    eng.wait_ge(sem, value)


def two_blocks(nc, x_in, slope, w_qk, w_kvu, w_out0, router0, gu0, down0, c0, wmod0,
               w_k, w_q, w_v, w_o, router1, gu1, down1, c1, wmod1, out, stop=9):
    S, D = x_in.shape
    NT = S // P
    KB = D // P
    CH = 512
    NC_ = S // CH
    TC = CH // P
    H0 = slope.shape[0]
    D0 = D // H0
    STRIP = 32
    HG = P // STRIP
    G0 = H0 // HG
    H1, _, DH = w_k.shape
    E = router0.shape[1]

    ctx = ExitStack()
    with ctx:
        def sem(name):
            return ctx.enter_context(nc.semaphore(name))

        def sb(name, shape, dt=F32, where=ctx):
            return where.enter_context(nc.sbuf_tensor(name, shape, dt))

        bank = [ctx.enter_context(nc.psum_tensor(f"bank{n}", [P, 512], F32)) for n in range(8)]
        WORK, SIDE = 4, 4

        x = sb("x", [P, NT, D])
        h_hi = sb("h_hi", [P, KB, S], F32R)
        h_lo = sb("h_lo", [P, KB, S], F32R)
        ident = sb("ident", [P, P])
        one = sb("one", [P, 1])
        spare = sb("spare", [P, 1])
        eps_ln = sb("eps_ln", [P, 1])
        eps_rms = sb("eps_rms", [P, 1])
        cols = [sb(f"cols{n}", [P, 4, KB]) for n in range(2)]
        gates = [sb(f"gates{n}", [P, 2, D]) for n in range(2)]
        stats = sb("stats", [P, NT, 6])
        msum = sb("msum", [P, NT])
        mdif = sb("mdif", [P, NT])
        vsum = sb("vsum", [P, NT])
        rstd = sb("rstd", [P, NT])
        comb = sb("comb", [P, NT, E + 1])

        def norm_buffers(where, tag):
            return (sb(f"xhat{tag}", [P, 2 * TC, D], where=where), sb(f"hf{tag}", [P, 4, CH], where=where))

        st = ExitStack()
        wmod = sb("wmod", [P, KB, 6 * D], where=st)
        cin = sb("cin", [P, KB], where=st)
        csil = sb("csil", [P, KB], where=st)
        cwide = sb("cwide", [P, KB, P], where=st)
        gabs = sb("gabs", [P, 2, D], where=st)
        gsgn = sb("gsgn", [P, 2, D], where=st)
        ones = sb("ones", [P, P], where=st)

        wqk = sb("wqk", [P, KB, 2 * D], where=st)
        wqk_hi = sb("wqk_hi", [P, KB, 2 * G0, P], F32R, where=st)
        wqk_lo = sb("wqk_lo", [P, KB, 2 * G0, P], F32R, where=st)
        wkvu = sb("wkvu", [P, KB, 3 * D], where=st)
        wkvu_hi = sb("wkvu_hi", [P, KB, 3 * D], F32R, where=st)
        wkvu_lo = sb("wkvu_lo", [P, KB, 3 * D], F32R, where=st)
        wo0 = sb("wo0", [P, KB, D], where=st)
        wo0_hi = sb("wo0_hi", [P, KB, D], F32R, where=st)
        wo0_lo = sb("wo0_lo", [P, KB, D], F32R, where=st)
        hc_hi = sb("hc_hi", [P, KB, CH], F32R, where=st)
        hc_lo = sb("hc_lo", [P, KB, CH], F32R, where=st)
        nslope = sb("nslope", [P, H0], where=st)
        nslope_s = sb("nslope_s", [P, G0], where=st)
        lag_i = sb("lag_i", [P, P], I32, where=st)
        lag = sb("lag", [P, P], where=st)
        rowi = sb("rowi", [P, P], I32, where=st)
        rowf = sb("rowf", [P, P], where=st)
        endi = sb("endi", [P, 1], I32, where=st)
        endf = sb("endf", [P, 1], where=st)
        decay = sb("decay", [P, HG, G0, P], where=st)
        qdec = sb("qdec", [P, G0, P], where=st)
        kdec = sb("kdec", [P, H0], where=st)
        bdec = sb("bdec", [P, G0], where=st)
        own = sb("own", [P, HG, D0], where=st)
        qT = sb("qT", [P, G0, CH], where=st)
        kT = sb("kT", [P, G0, CH], where=st)
        qdT = sb("qdT", [P, G0, CH], where=st)
        ksil = sb("ksil", [P, 2, D], where=st)
        kd = sb("kd", [P, 2, H0, STRIP], where=st)
        vt = sb("vt", [P, 2, D], where=st)
        ut = sb("ut", [P, 2, D], where=st)
        amat = sb("amat", [P, HG, G0, P], where=st)
        kv = sb("kv", [P, G0, HG * D0], where=st)
        kvn = sb("kvn", [P, G0, HG * D0], where=st)
        ou = sb("ou", [P, 2, D], where=st)
        osq = sb("osq", [P, D], where=st)
        ssq = sb("ssq", [P, TC], where=st)
        rms = sb("rms", [P, TC], where=st)
        oT_hi = sb("oT_hi", [P, TC, D], F32R, where=st)
        oT_lo = sb("oT_lo", [P, TC, D], F32R, where=st)
        xhat, hf = norm_buffers(st, "a")
        st.close()

        st = ExitStack()
        F_L = [down0.shape[1], down1.shape[1]]
        FT = -(-F_L[1] // P)
        FMAX = F_L[1]
        mgu = sb("mgu", [P, KB, 2 * FMAX], where=st)
        mdn = sb("mdn", [P, FT, D], where=st)
        gu_hi = [sb(f"gu_hi{n}", [P, KB, 2 * FMAX], F32R, where=st) for n in range(2)]
        gu_lo = [sb(f"gu_lo{n}", [P, KB, 2 * FMAX], F32R, where=st) for n in range(2)]
        dn_hi = [sb(f"dn_hi{n}", [P, FT, D], F32R, where=st) for n in range(2)]
        dn_lo = [sb(f"dn_lo{n}", [P, FT, D], F32R, where=st) for n in range(2)]
        HID = 8
        hid_hi = sb("hid_hi", [P, HID, CH], F32R, where=st)
        hid_lo = sb("hid_lo", [P, HID, CH], F32R, where=st)
        sil = sb("sil", [P, 2, CH], where=st)
        by_expert = sil
        ROUTED = 3
        hid = sb("hid", [P, 2, CH], where=st)
        rt = sb("rt", [P, KB, E], where=st)
        rt_hi = sb("rt_hi", [P, KB, E], F32R, where=st)
        rt_lo = sb("rt_lo", [P, KB, E], F32R, where=st)
        low = sb("low", [P, E, E], where=st)
        sc = sb("sc", [P, NT, E], where=st)
        rank = sb("rank", [P, NT, E], where=st)
        top = sb("top", [P, NT], where=st)
        den = sb("den", [P, NT], where=st)
        xhat_m, hf_m = norm_buffers(st, "m")
        gt = hf_m[:, 0:2, :].rearrange("p a (t e f) -> p (a t) e f", e=E, f=E)
        eq = hf_m[:, 2:4, :].rearrange("p a (t e f) -> p (a t) e f", e=E, f=E)
        st.close()

        st = ExitStack()
        KT_hi = sb("KT_hi", [P, S], F32R, where=st)
        KT_lo = sb("KT_lo", [P, S], F32R, where=st)
        QT_hi = sb("QT_hi", [P, 2, CH], F32R, where=st)
        QT_lo = sb("QT_lo", [P, 2, CH], F32R, where=st)
        V_hi = sb("V_hi", [P, NT, 2 * DH], F32R, where=st)
        V_lo = sb("V_lo", [P, NT, 2 * DH], F32R, where=st)
        SLOT = 4
        def row_width(q, r):
            return (q * TC + r + 1) * P

        def row_start(q, r):
            return sum(row_width(NC_ - 2 + q % 2, a) + SLOT for a in range(r))

        prob = [sb(f"prob{n}", [P, row_start(n, TC)], where=st) for n in range(2)]
        PTR = 3
        pT_hi = sb("pT_hi", [P, PTR, CH], F32R, where=st)
        pT_lo = sb("pT_lo", [P, PTR, CH], F32R, where=st)
        zT_hi = sb("zT_hi", [P, 2, CH], F32R, where=st)
        zT_lo = sb("zT_lo", [P, 2, CH], F32R, where=st)
        wkq = sb("wkq", [P, KB, 4 * DH], where=st)
        wkq_hi = sb("wkq_hi", [P, KB, 4 * DH], F32R, where=st)
        wkq_lo = sb("wkq_lo", [P, KB, 4 * DH], F32R, where=st)
        wv = sb("wv", [P, KB, 2 * DH], where=st)
        wv_hi = sb("wv_hi", [P, KB, 2 * DH], F32R, where=st)
        wv_lo = sb("wv_lo", [P, KB, 2 * DH], F32R, where=st)
        wo = sb("wo", [P, 2, D], where=st)
        wo_hi = sb("wo_hi", [P, 2, D], F32R, where=st)
        wo_lo = sb("wo_lo", [P, 2, D], F32R, where=st)
        negmask = sb("negmask", [P, P], where=st)
        nmax = sb("nmax", [P, NC_, TC], where=st)
        rsum = sb("rsum", [P, 2, NC_, TC], where=st)
        rinv = sb("rinv", [P, NC_, TC], where=st)
        xhat_s = prob[1][:, 0:8 * D].rearrange("p (t d) -> p t d", d=D)
        hf_s = prob[1][:, 8 * D:8 * D + 4 * CH].rearrange("p (t d) -> p t d", d=CH)
        st.close()

        work_full = sem("work_full")
        work_free = sem("work_free")
        x_loaded = [sem(f"x_loaded{c}") for c in range(NC_)]
        consts = sem("consts")
        c_loaded = sem("c_loaded")
        wmod_loaded = sem("wmod_loaded")
        c_silu = sem("c_silu")
        c_wide = sem("c_wide")
        mod_step = sem("mod_step")
        n_step = [sem(f"n_step{n}") for n in range(4)]
        n_std = [sem(f"n_std{n}") for n in range(4)]
        n_xhat = [sem(f"n_xhat{n}") for n in range(4)]
        n_lo = [sem(f"n_lo{n}") for n in range(4)]
        x_done = [sem(f"x_done{n}") for n in range(4)]
        a_loaded = [sem(f"a_loaded{n}") for n in range(5)]
        a_split = sem("a_split")
        a_tab = sem("a_tab")
        a_exp = sem("a_exp")
        a_sel = sem("a_sel")
        a_hc = sem("a_hc")
        a_silu = sem("a_silu")
        a_ks = sem("a_ks")
        a_kd = sem("a_kd")
        a_score = sem("a_score")
        a_mask = sem("a_mask")
        a_sq = sem("a_sq")
        a_kv = sem("a_kv")
        a_std = sem("a_std")
        a_rms = sem("a_rms")
        a_ohi = sem("a_ohi")
        m_rt = [sem(f"m_rt{n}") for n in range(2)]
        m_gu = [sem(f"m_gu{n}") for n in range(2)]
        m_dn = [sem(f"m_dn{n}") for n in range(2)]
        m_raw = [sem(f"m_raw{n}") for n in range(2)]
        m_zero = sem("m_zero")
        m_top = [sem(f"m_top{n}") for n in range(2)]
        m_scr = [sem(f"m_scr{n}") for n in range(2)]
        m_sce = [sem(f"m_sce{n}") for n in range(2)]
        m_sc = [sem(f"m_sc{n}") for n in range(2)]
        m_exp = [sem(f"m_exp{n}") for n in range(2)]
        m_sil = [sem(f"m_sil{n}") for n in range(2)]
        m_hi = [sem(f"m_hi{n}") for n in range(2)]
        m_lo = [sem(f"m_lo{n}") for n in range(2)]
        m_y = [sem(f"m_y{n}") for n in range(2)]
        s_w = sem("s_w")
        s_split = sem("s_split")
        s_neg = sem("s_neg")
        s_full = sem("s_full")
        s_free = sem("s_free")
        s_hi = sem("s_hi")
        s_row = sem("s_row")
        s_exp = sem("s_exp")
        s_pt = sem("s_pt")
        s_phi = sem("s_phi")
        s_plo = sem("s_plo")
        s_z = sem("s_z")
        s_zhi = sem("s_zhi")
        s_zlo = sem("s_zlo")
        s_inv = sem("s_inv")
        stored = sem("stored")

        block = ctx.enter_context(nc.Block())

        def mo(n):
            return ((xhat, hf), (xhat_m, hf_m), (xhat_s, hf_s), (xhat_m, hf_m))[n]

        XD = [1 + NT * a for a in (1, gu0.shape[0], H1, gu1.shape[0])]
        XD[2] = 2 + NT // 2 * H1
        A_EXPS = H0 + G0 + 2
        A_BASE = 2 * 2 + NC_ * KB
        A_WORK = 2 * G0 + 6 * TC
        A_TOKENS = 2 * G0 + 2 * TC + 2 + 3 * (TC - 3)
        S_RING = 3
        HEAD_WORK = 2 * NC_ + TC * sum(range(1, NC_ + 1)) + NT // 2
        PAIR_WORK = NT // 2 + 2 * HEAD_WORK
        PAIR_SPLIT, PAIR_LOADS = 10, 7 * 16
        HEAD_PT = sum(TC * (q + 1) for q in range(NC_))
        PT_RING, Z_BANK = 3, 6
        ORDER = [[("K", 0, 0)], [("Q", 0, 0)], [("Q", 0, 1)],
                 [("V", 0, 0), ("S", 0, 0)], [("Q", 0, 2)],
                 [("T", 0, 0), ("S", 0, 1)], [("Q", 0, 3)], [("Z", 0, 0)],
                 [("T", 0, 1), ("S", 0, 2)], [("Q", 1, 0)], [("O", 0, 0)], [("Z", 0, 1)],
                 [("T", 0, 2), ("S", 0, 3)], [("K", 1, 0)], [("Q", 1, 1)], [("O", 0, 1)], [("Z", 0, 2)],
                 [("T", 0, 3), ("S", 1, 0)], [("Q", 1, 2)], [("O", 0, 2)], [("Z", 0, 3)],
                 [("T", 1, 0), ("S", 1, 1)], [("Q", 1, 3)], [("O", 0, 3)], [("Z", 1, 0)],
                 [("T", 1, 1), ("S", 1, 2)], [("O", 1, 0)], [("Z", 1, 1)],
                 [("T", 1, 2), ("S", 1, 3)], [("O", 1, 1)], [("Z", 1, 2)],
                 [("T", 1, 3)], [("O", 1, 2)], [("Z", 1, 3)], [("O", 1, 3)]]
        IN_ORDER = [step for line in ORDER for step in line]
        EXP_MOST = 2 * CH
        INVERSES = 2 * sum(1 + (row_width(q, TC - 1) > EXP_MOST) for q in range(NC_))
        SOONER = 5
        AHEAD = 3

        def parts_of(what, q):
            return {"T": TC * (q + 1) + 1, "S": TC * (q + 1), "V": NT // 2}.get(what, 1)

        def take(steps, line):
            runs = [(steps[what](j, q), parts_of(what, q)) for what, j, q in line]
            pace = runs[0][1]
            over = max(1, pace - SOONER)
            for p in range(pace):
                next(runs[0][0])
                for run, n in runs[1:]:
                    for _ in range(min(n, -(-(p + 1) * n // over)) - min(n, -(-p * n // over))):
                        next(run)
            for run, _ in runs:
                for _ in run:
                    pass

        ROWS_BY = {}
        for what, j, q in IN_ORDER:
            if what == "S":
                ROWS_BY[j, q] = TC * (len(ROWS_BY) + 1)

        def work_of(what, q):
            return {"K": NC_, "Q": 1, "V": NT // 2, "S": TC * (q + 1), "T": 0, "Z": 0, "O": TC // 2}[what]

        def work_behind(n):
            return sum(work_of(what, q) for what, _, q in IN_ORDER[:n])

        assert work_behind(len(IN_ORDER)) == PAIR_WORK and PAIR_WORK % S_RING == 0
        m_tiles = [[(f * P, min(P, F - f * P)) for f in range(-(-F // P))] for F in F_L]
        m_banks = [[1 if 2 * w <= P else 2 for _, w in tiles] for tiles in m_tiles]
        m_count = [gu0.shape[0], gu1.shape[0]]
        m_base = [A_BASE + NC_ * A_WORK + NC_ * KB]
        m_base.append(m_base[0] + m_count[0] * sum(m_banks[0]) * NC_ + 2 * NC_ * KB)

        LEAD = [len(tiles) == 1 for tiles in m_tiles]

        def units(n, experts, front, back):
            for e, half, behind in experts:
                for c in range(NC_):
                    if not LEAD[n]:
                        front(e, half, c)
                    elif c < NC_ - 1:
                        front(e, half, c + 1)
                    elif behind:
                        front(e + 1, 1 - half, 0)
                    back(e, half, c)

        @block.sync
        def _(sp):
            sp.dma_start(cin[:, :], c0).then_inc(c_loaded, 16)
            sp.dma_start(wmod[:, :, :], wmod0.rearrange("(k p) n -> p k n", p=P)).then_inc(wmod_loaded, 16)
            for c in range(NC_):
                sp.dma_start(x[:, c * TC:(c + 1) * TC, :],
                             x_in[c * CH:(c + 1) * CH, :].rearrange("(t p) d -> p t d", p=P)).then_inc(x_loaded[c], 16)
            sp.dma_start(nslope[:, :], slope.rearrange("h a b -> (a b) h").to_broadcast([P, H0])).then_inc(a_loaded[3], 16)
            with nc.allow_non_contiguous_dma(reason="one slope for each strip"):
                for r in range(HG):
                    sp.dma_start(nslope_s[r * STRIP:(r + 1) * STRIP, :],
                                 slope[r::HG].rearrange("h a b -> (a b) h").to_broadcast([STRIP, G0])).then_inc(a_loaded[4], 16)
            sp.dma_start(wqk[:, :, :], w_qk.rearrange("(k p) n -> p k n", p=P)).then_inc(a_loaded[0], 16)
            sp.dma_start(wkvu[:, :, :], w_kvu.rearrange("(k p) n -> p k n", p=P)).then_inc(a_loaded[1], 16)
            sp.dma_start(wo0[:, :, :], w_out0.rearrange("(k p) n -> p k n", p=P)).then_inc(a_loaded[2], 16)
            sp.wait_ge(mod_step, 5)
            sp.dma_start(cin[:, :], c1).then_inc(c_loaded, 16)
            sp.dma_start(wmod[:, :, :], wmod1.rearrange("(k p) n -> p k n", p=P)).then_inc(wmod_loaded, 16)

            def load_expert(n, e, before, before_dn):
                gu, dn, F = (gu0, gu1)[n], (down0, down1)[n], F_L[n]
                wait(sp, m_raw[n], before)
                sp.dma_start(mgu[:, :, 0:2 * F], gu[bass.ds(e, 1), :, :].rearrange("a (k p) f -> p (a k) f", p=P)).then_inc(m_gu[n], 16)
                wait(sp, m_raw[n], before_dn)
                full = F // P
                if full:
                    sp.dma_start(mdn[:, 0:full, :], dn[bass.ds(e, 1), 0:full * P, :].rearrange("a (f p) d -> p (a f) d", p=P)).then_inc(m_dn[n], 16)
                sp.dma_start(mdn[0:F - full * P, full, :], dn[bass.ds(e, 1), full * P:F, :].rearrange("a p d -> (a p) d")).then_inc(m_dn[n], 16)

            def mixture(n):
                router = (router0, router1)[n]
                sp.wait_ge(x_done[2 * n], XD[2 * n])
                sp.dma_start(rt[:, :, :], router.rearrange("(k p) e -> p k e", p=P)).then_inc(m_rt[n], 16)
                load_expert(n, 0, 0, 0)
                rounds = (m_count[n] - 1) // 2
                with sp.Fori(0, rounds) as i:
                    for half in range(2):
                        load_expert(n, 2 * i + half + 1, i * 10 + 5 * half + 2, i * 10 + 5 * half + 5)
                if m_count[n] - 2 * rounds == 2:
                    load_expert(n, m_count[n] - 1, 10 * rounds + 2, 10 * rounds + 5)

            if stop >= 1:
                mixture(0)
            if stop >= 2:
                sp.wait_ge(x_done[1], XD[1])
                def load_pair(i):
                    for j in range(2):
                        for a, w in enumerate((w_k, w_q)):
                            sp.dma_start(wkq[:, :, (2 * j + a) * DH:(2 * j + a + 1) * DH],
                                         w[bass.ds(2 * i + j, 1), :, :].rearrange("a (k p) h -> p (a k) h", p=P)).then_inc(s_w, 16)
                        sp.dma_start(wv[:, :, j * DH:(j + 1) * DH],
                                     w_v[bass.ds(2 * i + j, 1), :, :].rearrange("a (k p) h -> p (a k) h", p=P)).then_inc(s_w, 16)
                    sp.dma_start(wo[:, :, :], w_o[bass.ds(2 * i, 2), :, :].rearrange("a p d -> p a d")).then_inc(s_w, 16)

                load_pair(0)
                with sp.Fori(0, H1 // 2 - 1) as i:
                    sp.wait_ge(s_split, i * PAIR_SPLIT + PAIR_SPLIT)
                    load_pair(i + 1)
            if stop >= 3:
                mixture(1)
            last = min(stop, 3)
            sp.wait_ge(x_done[last], XD[last])
            for c in range(NC_):
                sp.dma_start(out[c * CH:(c + 1) * CH, :].rearrange("(t p) d -> p t d", p=P),
                             x[:, c * TC:(c + 1) * TC, :]).then_inc(stored, 16)
            sp.wait_ge(stored, 16 * NC_)

        @block.gpsimd
        def _(pool):
            def rounded(out_, in_):
                ones_ = one[:, :].rearrange("p (a b) -> p a b", a=1).to_broadcast(list(in_.shape))
                return pool.tensor_tensor(out_, in_, ones_, ALU.mult)

            pool.memset(ident[:, :], 0.0).then_inc(consts, 1)
            pool.memset(ones[:, :], 1.0).then_inc(consts, 1)
            pool.memset(eps_ln[:, :], LN_EPS).then_inc(consts, 1)
            pool.memset(eps_rms[:, :], RMS_EPS).then_inc(consts, 1)
            pool.memset(one[:, :], 1.0).then_inc(a_split, 1)
            pool.wait_ge(consts, 4)
            pool.affine_select(out=ident[:, :], in_=ident[:, :], compare_op=ALU.not_equal, fill=1.0,
                               base=0, pattern=[[-1, P]], channel_multiplier=1).then_inc(consts, 1)
            pool.iota(lag_i[:, :], pattern=[[1, P]], base=0, channel_multiplier=-1).then_inc(consts, 1)
            pool.iota(rowi[:, :], pattern=[[1, P]], base=1, channel_multiplier=0).then_inc(consts, 1)
            pool.iota(endi[:, :], pattern=[[0, 1]], base=P - 1, channel_multiplier=-1).then_inc(consts, 1)
            pool.memset(own[:, :, :], 1.0).then_inc(consts, 1)
            pool.wait_ge(consts, 9)
            pool.affine_select(out=own[:, :, :], in_=own[:, :, :], compare_op=ALU.is_ge, fill=0.0,
                               base=0, pattern=[[-STRIP, HG], [0, D0]], channel_multiplier=1).then_inc(consts, 1)
            pool.wait_ge(consts, 10)
            pool.affine_select(out=own[:, :, :], in_=own[:, :, :], compare_op=ALU.is_ge, fill=0.0,
                               base=D0 - 1, pattern=[[STRIP, HG], [0, D0]], channel_multiplier=-1).then_inc(consts, 1)
            for t in (wqk_hi, wqk_lo):
                pool.memset(t[:, :, :, :].bitcast(F32), 0.0).then_inc(a_split, 1)
            pool.memset(kd[:, :, :, :], 0.0).then_inc(a_sel, 1)
            pool.wait_ge(a_split, 3)
            pool.wait_ge(a_loaded[0], 16)
            for k in range(KB):
                raw = wqk[:, k, :].rearrange("p (g r d) -> p g r d", r=HG, d=D0)
                hi = wqk_hi[:, k, :, :].rearrange("p g (r s) -> p g r s", s=STRIP)[:, :, :, 0:D0]
                lo = wqk_lo[:, k, :, :].rearrange("p g (r s) -> p g r s", s=STRIP)[:, :, :, 0:D0]
                pool.tensor_copy(hi, raw).then_inc(a_split, 1)
                pool.wait_ge(a_split, 4 + 2 * k)
                pool.tensor_tensor(lo, raw, hi.bitcast(F32), ALU.subtract).then_inc(a_split, 1)
            pool.wait_ge(a_loaded[1], 16)
            pool.tensor_copy(wkvu_hi[:, :, :], wkvu[:, :, :]).then_inc(a_split, 1)
            pool.wait_ge(a_split, 8)
            pool.tensor_tensor(wkvu_lo[:, :, :], wkvu[:, :, :], wkvu_hi[:, :, :].bitcast(F32), ALU.subtract).then_inc(a_split, 1)
            pool.wait_ge(a_loaded[2], 16)
            pool.wait_ge(mod_step, 5)
            for k in range(KB):
                pool.tensor_tensor(wo0[:, k, :], wo0[:, k, :], gates[0][:, 0, :], ALU.mult).then_inc(a_split, 1)
            pool.wait_ge(a_split, 11)
            pool.tensor_copy(wo0_hi[:, :, :], wo0[:, :, :]).then_inc(a_split, 1)
            pool.wait_ge(a_split, 12)
            pool.tensor_tensor(wo0_lo[:, :, :], wo0[:, :, :], wo0_hi[:, :, :].bitcast(F32), ALU.subtract).then_inc(a_split, 1)
            pool.wait_ge(a_exp, H0)
            pool.affine_select(out=decay[:, :, :, :].rearrange("p r g m -> p (r g) m"),
                               in_=decay[:, :, :, :].rearrange("p r g m -> p (r g) m"),
                               compare_op=ALU.is_ge, fill=0.0, base=0,
                               pattern=[[0, H0], [1, P]], channel_multiplier=-1).then_inc(a_sel, 1)
            with pool.Fori(0, NC_) as i:
                pool.wait_ge(n_lo[0], KB * i + KB)
                pool.wait_ge(work_full, i * A_WORK + (A_BASE - A_WORK + A_TOKENS))
                for k in range(KB):
                    pool.tensor_copy(hc_hi[:, k, :], h_hi[:, k, bass.ds(i * CH, CH)]).then_inc(a_hc, 1)
                    pool.tensor_copy(hc_lo[:, k, :], h_lo[:, k, bass.ds(i * CH, CH)]).then_inc(a_hc, 1)

            def split_expert(n, half, at, loads):
                F, tiles = F_L[n], m_tiles[n]
                nt, dmas = len(tiles), 1 + (F_L[n] >= P)
                pool.wait_ge(m_gu[n], loads * 16)
                rounded(gu_hi[half][:, :, 0:2 * F], mgu[:, :, 0:2 * F]).then_inc(m_raw[n], 1)
                pool.wait_ge(m_raw[n], at + 1)
                pool.tensor_tensor(gu_lo[half][:, :, 0:2 * F], mgu[:, :, 0:2 * F],
                                   gu_hi[half][:, :, 0:2 * F].bitcast(F32), ALU.subtract).then_inc(m_raw[n], 1)
                pool.wait_ge(m_dn[n], loads * 16 * dmas)
                pool.wait_ge(m_raw[n], at + 2)
                pool.tensor_tensor(mdn[:, 0:nt, :], mdn[:, 0:nt, :],
                                   gates[n][:, 1:2, :].to_broadcast([P, nt, D]), ALU.mult).then_inc(m_raw[n], 1)
                pool.wait_ge(m_raw[n], at + 3)
                rounded(dn_hi[half][:, 0:nt, :], mdn[:, 0:nt, :]).then_inc(m_raw[n], 1)
                pool.wait_ge(m_raw[n], at + 4)
                pool.tensor_tensor(dn_lo[half][:, 0:nt, :], mdn[:, 0:nt, :],
                                   dn_hi[half][:, 0:nt, :].bitcast(F32), ALU.subtract).then_inc(m_raw[n], 1)

            def mixture(n):
                pool.wait_ge(x_done[2 * n], XD[2 * n])
                F, tiles = F_L[n], m_tiles[n]
                last = len(tiles) - 1
                pad = tiles[-1][1]
                zeroed = 5 * n
                pool.memset(low[:, :, :], 1.0).then_inc(m_zero, 1)
                for b in (mdn[pad:P, last, :], hid_hi[pad:P, :, :].bitcast(F32), hid_lo[pad:P, :, :].bitcast(F32)):
                    zeroed += 1
                    pool.wait_ge(m_zero, zeroed)
                    pool.memset(b, 0.0).then_inc(m_zero, 1)
                pool.wait_ge(m_zero, zeroed + 1)
                pool.affine_select(out=low[:, :, :], in_=low[:, :, :], compare_op=ALU.is_gt, fill=0.0,
                                   base=0, pattern=[[1, E], [-1, E]], channel_multiplier=0).then_inc(m_zero, 1)
                pool.wait_ge(m_zero, zeroed + 2)
                split_expert(n, 0, 0, 1)
                T = m_count[n]
                rounds = (T - 1) // 2
                uses = sum(m_banks[n]) * NC_
                begun = m_base[n] + 1 + LEAD[n] * sum(m_banks[n])
                with pool.Fori(0, rounds) as i:
                    pool.wait_ge(work_full, i * 2 * uses + begun)
                    split_expert(n, 1, i * 10 + 5, 2 * i + 2)
                    pool.wait_ge(work_full, i * 2 * uses + begun + uses)
                    split_expert(n, 0, i * 10 + 10, 2 * i + 3)
                if T - 2 * rounds == 2:
                    pool.wait_ge(work_full, rounds * 2 * uses + begun)
                    split_expert(n, 1, rounds * 10 + 5, T)

            if stop >= 1:
                mixture(0)
            if stop >= 2:
                pool.wait_ge(x_done[1], XD[1])
                pool.memset(negmask[:, :], 0.0).then_inc(s_neg, 1)
                pool.wait_ge(s_neg, 1)
                pool.affine_select(out=negmask[:, :], in_=negmask[:, :], compare_op=ALU.is_ge, fill=MASKED,
                                   base=0, pattern=[[-1, P]], channel_multiplier=1).then_inc(s_neg, 1)
                after = {(what, j, q): work_behind(n + 1) for n, (what, j, q) in enumerate(IN_ORDER)}

                def split_pair(pair, used):
                    at = pair * PAIR_SPLIT
                    pool.wait_ge(s_w, pair * PAIR_LOADS + PAIR_LOADS)

                    def split(hi, lo, raw, step):
                        rounded(hi, raw).then_inc(s_split, 1)
                        pool.wait_ge(s_split, at + step + 1)
                        pool.tensor_tensor(lo, raw, hi.bitcast(F32), ALU.subtract).then_inc(s_split, 1)

                    used(max(after["V", 0, 0], after["S", 0, 0]))
                    split(wv_hi[:, :, :], wv_lo[:, :, :], wv[:, :, :], 0)
                    for j in range(2):
                        used(after["Q", j, NC_ - 1])
                        c = slice(2 * j * DH, (2 * j + 2) * DH)
                        split(wkq_hi[:, :, c], wkq_lo[:, :, c], wkq[:, :, c], 2 + 2 * j)
                    for j in range(2):
                        pool.tensor_tensor(wo[:, j, :], wo[:, j, :], gates[1][:, 0, :], ALU.mult).then_inc(s_split, 1)
                    pool.wait_ge(s_split, at + 8)
                    used(PAIR_WORK)
                    split(wo_hi[:, :, :], wo_lo[:, :, :], wo[:, :, :], 8)

                split_pair(0, lambda work: None)
                with pool.Fori(0, H1 // 2 - 1) as i:
                    split_pair(i + 1, lambda work: pool.wait_ge(s_full, i * PAIR_WORK + work))
            if stop >= 3:
                mixture(1)

        @block.vector
        def _(dve):
            work = Turn()

            def modulation(n):
                dve.wait_ge(c_silu, n + 1)
                dve.wait_ge(consts, 2)
                if n:
                    dve.wait_ge(work_full, 2)
                for k in range(KB):
                    dve.tensor_scalar(cwide[:, k, :], ones[:, :], csil[:, k:k + 1], None, ALU.mult).then_inc(c_wide, 1)
                at = work.next()
                dve.wait_ge(work_full, at + 1)
                dve.tensor_copy(cols[n][:, :, :].rearrange("p v k -> p (v k)"), bank[at % WORK][:, 0:4 * KB]).then_inc(work_free, 1)
                dve.wait_ge(work_free, at + 1)
                dve.tensor_scalar(cols[n][:, 1::2, :], cols[n][:, 1::2, :], 1.0, None, ALU.add).then_inc(mod_step, 1)
                at = work.next()
                dve.wait_ge(work_full, at + 1)
                g = gates[n][:, :, :]
                dve.tensor_copy(g, bank[at % WORK][:, 0:2 * D].rearrange("p (a d) -> p a d", a=2)).then_inc(work_free, 1)
                dve.wait_ge(work_free, at + 1)
                dve.tensor_scalar(gsgn[:, :, :], g, 0.0, 2.0, ALU.is_ge, ALU.mult).then_inc(mod_step, 1)
                dve.scalar_tensor_tensor(gabs[:, :, :], g, -1.0, g, ALU.mult, ALU.max).then_inc(mod_step, 1)
                dve.wait_ge(mod_step, 5 * n + 3)
                dve.tensor_scalar(gabs[:, :, :], gabs[:, :, :], LEAST_GATE, None, ALU.max).then_inc(mod_step, 1)
                dve.wait_ge(mod_step, 5 * n + 4)
                dve.scalar_tensor_tensor(g, gsgn[:, :, :], -1.0, gabs[:, :, :], ALU.add, ALU.mult).then_inc(mod_step, 1)

            def statistics(n, tiles):
                for t in tiles:
                    if n == 0 and t % TC == 0:
                        dve.wait_ge(x_loaded[t // TC], 16)
                    dve.bn_stats(stats[:, t, :], x[:, t, :]).then_inc(n_step[n], 1)

            def norm(n, known=0):
                xh, hfb = mo(n)
                if n:
                    dve.wait_ge(x_done[n - 1], XD[n - 1])
                statistics(n, range(known, NT))
                dve.wait_ge(n_step[n], NT)
                dve.tensor_tensor(msum[:, :], stats[:, :, 1], stats[:, :, 4], ALU.add).then_inc(n_step[n], 1)
                dve.tensor_tensor(mdif[:, :], stats[:, :, 1], stats[:, :, 4], ALU.subtract).then_inc(n_step[n], 1)
                dve.tensor_tensor(vsum[:, :], stats[:, :, 2], stats[:, :, 5], ALU.add).then_inc(n_step[n], 1)
                dve.wait_ge(n_step[n], NT + 3)
                dve.tensor_tensor(mdif[:, :], mdif[:, :], mdif[:, :], ALU.mult).then_inc(n_step[n], 1)
                dve.tensor_scalar(msum[:, :], msum[:, :], 0.5, None, ALU.mult).then_inc(n_step[n], 1)
                dve.wait_ge(n_step[n], NT + 4)
                dve.scalar_tensor_tensor(vsum[:, :], mdif[:, :], D / 4, vsum[:, :], ALU.mult, ALU.add).then_inc(n_step[n], 1)
                dve.wait_ge(n_std[n], 1)
                dve.reciprocal(rstd[:, :], rstd[:, :]).then_inc(n_step[n], 1)
                dve.wait_ge(n_step[n], NT + 7)
                if n % 2:
                    split_router(n // 2)
                first = work.at()
                lo_of = lambda u: (h_lo[:, u % KB, u // KB * CH:(u // KB + 1) * CH], h_hi[:, u % KB, u // KB * CH:(u // KB + 1) * CH])

                def lo_part(u):
                    lo, hi = lo_of(u)
                    dve.wait_ge(work_free, work.next() + 1)
                    dve.tensor_tensor(lo, hfb[:, u % 4, :], hi.bitcast(F32), ALU.subtract).then_inc(n_lo[n], 1)

                def turned(c):
                    for k in range(KB):
                        lo_part(c * KB + k)

                for c in range(NC_):
                    if c >= 2:
                        dve.wait_ge(work_full, first + KB * (c - 1))
                    for t in range(c * TC, (c + 1) * TC):
                        dve.tensor_scalar(xh[:, t % (2 * TC), :], x[:, t, :], msum[:, t:t + 1], rstd[:, t:t + 1],
                                          ALU.subtract, ALU.mult).then_inc(n_xhat[n], 1)
                    if c >= 2:
                        turned(c - 2)
                turned(NC_ - 2)
                turned(NC_ - 1)

            def split_router(n):
                dve.wait_ge(m_rt[n], 16)
                dve.tensor_copy(rt_hi[:, :, :], rt[:, :, :]).then_inc(m_top[n], 1)
                dve.wait_ge(m_top[n], 1)
                dve.tensor_tensor(rt_lo[:, :, :], rt[:, :, :], rt_hi[:, :, :].bitcast(F32), ALU.subtract).then_inc(m_top[n], 1)

            def tables():
                dve.wait_ge(consts, 8)
                dve.tensor_copy(lag[:, :], lag_i[:, :]).then_inc(a_tab, 1)
                dve.tensor_copy(rowf[:, :], rowi[:, :]).then_inc(a_tab, 1)
                dve.tensor_copy(endf[:, :], endi[:, :]).then_inc(a_tab, 1)
                dve.wait_ge(a_loaded[3], 16)
                dve.tensor_scalar(nslope[:, :], nslope[:, :], -1.0, None, ALU.mult).then_inc(a_tab, 1)
                dve.wait_ge(a_loaded[4], 16 * HG)
                dve.tensor_scalar(nslope_s[:, :], nslope_s[:, :], -1.0, None, ALU.mult).then_inc(a_tab, 1)
                dve.wait_ge(a_tab, 5)
                dve.tensor_scalar(lag[:, :], lag[:, :], 0.0, None, ALU.max).then_inc(a_tab, 1)

            def linear_attention():
                dve.wait_ge(a_exp, A_EXPS)
                dve.wait_ge(a_sel, 2)
                dve.memset(kv[:, :, :], 0.0).then_inc(a_kv, G0)
                with dve.Fori(0, NC_) as i:
                    work.enter(i, A_WORK)
                    token = lambda t: i * TC + t

                    for g in range(G0):
                        work.next()
                        work.next()
                        dve.wait_ge(a_silu, i * 2 * G0 + 2 * g + 2)
                        dve.tensor_tensor(qdT[:, g, :].rearrange("p (t m) -> p t m", m=P), qT[:, g, :].rearrange("p (t m) -> p t m", m=P),
                                          qdec[:, g:g + 1, :].to_broadcast([P, TC, P]), ALU.mult).then_inc(work_free, 2)

                    def by_token(t):
                        at = work.next()
                        dve.wait_ge(a_ks, token(t) + 1)
                        dve.tensor_tensor(kd[:, t % 2, :, 0:D0], ksil[:, t % 2, :].rearrange("p (h d) -> p h d", d=D0),
                                          kdec[:, :].rearrange("p (h a) -> p h a", a=1).to_broadcast([P, H0, D0]), ALU.mult).then_inc(a_kd, 1)
                        dve.tensor_copy(vt[:, t % 2, :], bank[(work.fixed - 1) % WORK][:, D:2 * D]).then_inc(work_free, 1)
                        work.next()
                        dve.wait_ge(work_full, at + 2)
                        dve.tensor_copy(ut[:, t % 2, :], bank[(work.fixed - 1) % WORK][:, 0:D]).then_inc(work_free, 1)

                    def out_lo(t):
                        at = work.next()
                        dve.wait_ge(a_ohi, token(t) + 1)
                        dve.tensor_tensor(oT_lo[:, t, :], bank[(work.fixed - 1) % WORK][:, 0:D], oT_hi[:, t, :].bitcast(F32),
                                          ALU.subtract).then_inc(work_free, 1)

                    by_token(0)
                    for t in range(TC):
                        for r in range(HG):
                            dve.wait_ge(a_score, token(t) * HG + r + 1)
                            dve.tensor_tensor(amat[:, r, :, :], bank[SIDE + r][:, :].rearrange("p (g m) -> p g m", m=P),
                                              decay[:, r, :, :], ALU.mult).then_inc(a_mask, 1)
                        if t < TC - 1:
                            by_token(t + 1)
                        if t >= 1:
                            out_lo(t - 1)
                        at = work.next()
                        dve.wait_ge(a_sq, token(t) + 1)
                        dve.tensor_tensor(ou[:, t % 2, :], bank[(work.fixed - 1) % WORK][:, 0:D], ut[:, t % 2, :],
                                          ALU.mult).then_inc(work_free, 1)
                        at = work.next()
                        dve.wait_ge(work_full, at + 1)
                        dve.tensor_tensor(kvn[:, :, :].rearrange("p g (r d) -> p g r d", d=D0),
                                          bank[(work.fixed - 1) % WORK][:, 0:D].rearrange("p (g r d) -> p g r d", r=HG, d=D0),
                                          own[:, :, :].rearrange("p (a r) d -> p a r d", a=1).to_broadcast([P, G0, HG, D0]),
                                          ALU.mult).then_inc(work_free, 1)
                        dve.wait_ge(work_free, at + 1)
                        dve.wait_ge(a_kv, token(t) * G0 + G0)
                        for g in range(G0):
                            dve.scalar_tensor_tensor(kv[:, g, :], kv[:, g, :], bdec[:, g:g + 1], kvn[:, g, :],
                                                     ALU.mult, ALU.add).then_inc(a_kv, 1)
                    out_lo(TC - 1)
                    dve.wait_ge(a_std, i + 1)
                    dve.reciprocal(rms[:, :], rms[:, :]).then_inc(a_rms, 1)
                    dve.wait_ge(a_rms, i + 1)
                    for t in range(TC):
                        at = work.next()
                        dve.wait_ge(work_full, at + 1)
                        xt = x[:, bass.ds(i * TC + t, 1), :].rearrange("p a d -> p (a d)")
                        dve.scalar_tensor_tensor(xt, bank[(work.fixed - 1) % WORK][:, 0:D], rms[:, t:t + 1], xt,
                                                 ALU.mult, ALU.add).then_inc(work_free, 1)
                work.leave(NC_)
                dve.wait_ge(work_free, work.at())
                dve.tensor_copy(rms[:, 0:1], ssq[:, 0:1]).then_inc(x_done[0], XD[0])

            def mixture(n):
                F, tiles, T = F_L[n], m_tiles[n], m_count[n]
                step = [2]

                def done(ins):
                    step[0] += 1
                    ins.then_inc(m_top[n], 1)
                    dve.wait_ge(m_top[n], step[0])

                dve.wait_ge(m_sc[n], NC_)
                done(dve.tensor_copy(sc[:, :, :].rearrange("p t e -> p (t e)"), bank[SIDE][:, 0:NT * E]))
                done(dve.tensor_reduce(top[:, :], sc[:, :, :], AX.X, ALU.max))
                row = sc[:, :, :].rearrange("p t (a e) -> p t a e", a=1).to_broadcast([P, NT, E, E])
                col = sc[:, :, :].rearrange("p t (e a) -> p t e a", a=1).to_broadcast([P, NT, E, E])
                done(dve.tensor_tensor(gt, row, col, ALU.is_gt))
                done(dve.tensor_tensor(eq, row, col, ALU.is_equal))
                dve.wait_ge(m_zero, 5 * n + 5)
                done(dve.tensor_tensor(eq, eq, low[:, :, :].rearrange("p (a e) f -> p a e f", a=1).to_broadcast([P, NT, E, E]), ALU.mult))
                done(dve.tensor_tensor(gt, gt, eq, ALU.add))
                done(dve.tensor_reduce(rank[:, :, :], gt, AX.X, ALU.add))
                done(dve.tensor_tensor(sc[:, :, :], sc[:, :, :], top[:, :].rearrange("p (t a) -> p t a", a=1).to_broadcast([P, NT, E]),
                                       ALU.subtract))
                dve.wait_ge(m_exp[n], 1)
                done(dve.scalar_tensor_tensor(comb[:, :, 0:E], rank[:, :, :], 2.0, sc[:, :, :], ALU.is_lt, ALU.mult))
                done(dve.tensor_reduce(den[:, :], comb[:, :, 0:E], AX.X, ALU.add))
                done(dve.reciprocal(den[:, :], den[:, :]))
                done(dve.tensor_tensor(comb[:, :, 0:E], comb[:, :, 0:E],
                                       den[:, :].rearrange("p (t a) -> p t a", a=1).to_broadcast([P, NT, E]), ALU.mult))
                done(dve.memset(comb[:, :, E:E + 1], 1.0))
                dve.memset(spare[:, :], 0.0).then_inc(x_done[2 * n + 1], 1)

                tile, y, added = Turn(), Turn(), Turn()
                nf = len(tiles)

                def lo_part(w):
                    u = lo.next()
                    s = (lo.fixed - 1) % HID
                    dve.wait_ge(m_hi[n], u + 1)
                    dve.tensor_tensor(hid_lo[0:w, s, :], hid[0:w, (lo.fixed - 1) % 2, :], hid_hi[0:w, s, :].bitcast(F32),
                                      ALU.subtract).then_inc(m_lo[n], 1)

                def front(e, half, c):
                    for f, (f0, w) in enumerate(tiles):
                        u, banks = tile.next(), m_banks[n][f]
                        at = [work.next() for _ in range(banks)][-1]
                        dve.wait_ge(m_sil[n], u + 1)
                        dve.wait_ge(work_full, at + 1)
                        if f == 0:
                            dve.wait_ge(x_done[2 * n + 1], added.at() + 1)
                        elif f > 1:
                            dve.wait_ge(m_lo[n], u - 1)
                        dve.tensor_tensor(hid[0:w, (tile.fixed - 1) % 2, :], bank[(work.fixed - 1) % WORK][0:w, :],
                                          sil[0:w, (tile.fixed - 1) % 2, :], ALU.mult).then_inc(work_free, banks)
                        if f:
                            lo_part(tiles[f - 1][1])
                    lo_part(tiles[-1][1])

                def back(e, half, c):
                    dve.wait_ge(x_done[2 * n + 1], added.at() + 1)
                    for t in range(TC):
                        if t % 2 == 0:
                            yu = y.next()
                            dve.wait_ge(m_y[n], yu + 1)
                        added.next()
                        k = c * TC + t
                        dve.scalar_tensor_tensor(x[:, k, :], bank[SIDE + (y.fixed - 1) % 4][:, t % 2 * D:(t % 2 + 1) * D],
                                                 comb[:, k, bass.ds(e, 1)], x[:, k, :], ALU.mult, ALU.add).then_inc(x_done[2 * n + 1], 1)
                    if n == 0 and isinstance(e, int) and e == T - 1 and c < NC_ - 1:
                        dve.wait_ge(x_done[2 * n + 1], added.at() + 1)
                        statistics(2, range(c * TC, (c + 1) * TC))

                lo = Turn()
                rounds = (T - 1) // 2
                if LEAD[n]:
                    front(0, 0, 0)
                with dve.Fori(0, rounds) as i:
                    for turn, per in ((work, sum(m_banks[n]) * NC_), (tile, nf * NC_), (lo, nf * NC_), (y, 2 * NC_), (added, NT)):
                        turn.enter(i, 2 * per)
                    units(n, [(2 * i + half, half, True) for half in range(2)], front, back)
                for turn in (work, tile, lo, y, added):
                    turn.leave(rounds)
                units(n, [(e, e % 2, e < T - 1) for e in range(2 * rounds, T)], front, back)

            def softmax_attention():
                work_s, pt, added = Turn(), Turn(), Turn()
                rows = Turn()
                z = Turn()
                his = Turn()
                inverses = Turn()
                dve.memset(rinv[:, :, :], 0.0).then_inc(s_free, S_RING)
                dve.memset(spare[:, :], 0.0).then_inc(x_done[2], 1)
                dve.wait_ge(s_neg, 2)

                def projected(lo, hi, scale=None):
                    u, b = work_s.next(), bank[(work_s.fixed - 1) % S_RING]
                    dve.wait_ge(s_hi, his.next() + 1)
                    src = b[:, :]
                    if len(lo.shape) == 3:
                        src = src.rearrange("p (t h) -> p t h", t=2)
                    if scale is None:
                        dve.tensor_tensor(lo, src, hi.bitcast(F32), ALU.subtract).then_inc(s_free, 1)
                    else:
                        dve.scalar_tensor_tensor(lo, src, scale, hi.bitcast(F32), ALU.mult, ALU.subtract).then_inc(s_free, 1)

                def keys(j, q):
                    for c in range(NC_):
                        projected(KT_lo[:, c * CH:(c + 1) * CH], KT_hi[:, c * CH:(c + 1) * CH])
                    yield

                def queries(j, q):
                    projected(QT_lo[:, q % 2, :], QT_hi[:, q % 2, :], DH ** -0.5)
                    yield

                def values(j, q):
                    for t in range(0, NT, 2):
                        projected(V_lo[:, t:t + 2, :], V_hi[:, t:t + 2, :])
                        yield

                def scores(j, q):
                    p = prob[q % 2]
                    for r in range(TC):
                        at0, width = row_start(q, r), row_width(q, r)
                        for c in range(q + 1):
                            u, b = work_s.next(), bank[(work_s.fixed - 1) % S_RING]
                            dve.wait_ge(s_full, u + 1)
                            n = CH if c < q else r * P
                            if n:
                                ins = dve.tensor_scalar(p[:, at0 + c * CH:at0 + c * CH + n], b[:, 0:n], 1.0, LOWEST, ALU.mult, ALU.max,
                                                        accum_out=p[:, at0 + width + c:at0 + width + c + 1])
                            if c < q:
                                ins.then_inc(s_free, 1)
                            else:
                                dve.tensor_tensor(p[:, at0 + width - P:at0 + width], b[:, n:n + P], negmask[:, :], ALU.add).then_inc(s_free, 1)
                                dve.wait_ge(s_free, u + 1 + S_RING)
                                rows.next()
                                dve.tensor_reduce(nmax[:, q, r:r + 1], p[:, at0 + width - P:at0 + width + q + (r > 0)], AX.X,
                                                  ALU.max, negate=True).then_inc(s_row, 1)
                            yield

                def turned(j, q):
                    for kt in range(TC * (q + 1)):
                        if kt >= AHEAD:
                            yield
                        r0 = max(0, kt - TC * q) * P
                        u, s = pt.next(), kt % PTR
                        dve.wait_ge(s_phi, u + 1)
                        dve.tensor_tensor(pT_lo[:, s, r0:CH], bank[S_RING + s][:, r0:CH], pT_hi[:, s, r0:CH].bitcast(F32),
                                          ALU.subtract).then_inc(s_plo, 1)
                    for _ in range(AHEAD + 1):
                        yield

                def head_out(j, q):
                    dve.wait_ge(s_zhi, z.next() + 1)
                    dve.tensor_tensor(zT_lo[:, q % 2, :], bank[Z_BANK + q % 2][:, :], zT_hi[:, q % 2, :].bitcast(F32),
                                      ALU.subtract).then_inc(s_zlo, 1)
                    yield

                def outputs(j, q):
                    dve.wait_ge(s_exp, ROWS_BY[j, q] + rounds_rows())
                    first = next(r for r in range(TC + 1) if r == TC or row_width(q, r) > EXP_MOST)
                    if first < TC:
                        dve.tensor_tensor(rsum[:, 0, q, first:TC], rsum[:, 0, q, first:TC], rsum[:, 1, q, first:TC], ALU.add).then_inc(s_inv, 1)
                        dve.wait_ge(s_inv, inverses.next() + 1)
                    dve.reciprocal(rinv[:, q, :], rsum[:, 0, q, :]).then_inc(s_inv, 1)
                    dve.wait_ge(s_inv, inverses.next() + 1)
                    dve.wait_ge(x_done[2], added.at() + 1)
                    dve.wait_ge(s_free, work_s.at() + S_RING)
                    for t in range(TC):
                        if t % 2 == 0:
                            u = work_s.next()
                            dve.wait_ge(s_full, u + 1)
                            b = bank[(work_s.fixed - 1) % S_RING]
                        k = q * TC + t
                        ins = dve.scalar_tensor_tensor(x[:, k, :], b[:, t % 2 * D:(t % 2 + 1) * D], rinv[:, q, t:t + 1], x[:, k, :],
                                                       ALU.mult, ALU.add)
                        if t % 2:
                            ins.then_inc(s_free, 1)
                        else:
                            added.next()
                            ins.then_inc(x_done[2], 1)
                    yield

                steps = {"K": keys, "Q": queries, "V": values, "S": scores, "T": turned, "Z": head_out, "O": outputs}
                with dve.Fori(0, H1 // 2) as i:
                    rounds_rows = lambda: i * (2 * NT)
                    work_s.enter(i, PAIR_WORK)
                    for turn, per in ((pt, 2 * HEAD_PT), (added, NT), (rows, 2 * NT), (z, 2 * NC_),
                                      (his, NT // 2 + 4 * NC_), (inverses, INVERSES)):
                        turn.enter(i, per)
                    for line in ORDER:
                        take(steps, line)
                for turn in (work_s, pt, added, rows, z, his, inverses):
                    turn.leave(H1 // 2)
                dve.wait_ge(s_free, work_s.at() + S_RING)
                dve.memset(spare[:, :], 0.0).then_inc(x_done[2], 1)

            statistics(0, range(NT))
            modulation(0)
            norm(0, NT)
            tables()
            modulation(1)
            linear_attention()
            if stop >= 1:
                norm(1)
                mixture(0)
            if stop >= 2:
                norm(2, NT - TC)
                softmax_attention()
            if stop >= 3:
                norm(3)
                mixture(1)

        @block.scalar
        def _(act):
            work = Turn()
            def modulation(n):
                act.wait_ge(c_loaded, 16 * (n + 1))
                if n:
                    act.wait_ge(c_wide, KB)
                act.activation(csil[:, :], cin[:, :], ACT.Silu).then_inc(c_silu, 1)
                work.fixed += 2

            def norm(n):
                _, hfb = mo(n)
                layer, v = n // 2, 2 * (n % 2)
                act.wait_ge(n_step[n], NT + 6)
                act.activation(rstd[:, :], vsum[:, :], ACT.Sqrt, scale=1.0 / D, bias=eps_ln[:, :]).then_inc(n_std[n], 1)
                def by_expert_out(c):
                    m = n // 2
                    act.wait_ge(m_scr[m], c + 1)
                    if c >= 2:
                        act.wait_ge(m_sc[m], c - 1)
                    act.activation(by_expert[0:E, c % 2, :], bank[SIDE + 1 + c % ROUTED][0:E, :], ACT.Copy).then_inc(m_sce[m], 1)

                for u in range(NC_ * KB):
                    k, at = u % KB, work.next()
                    scale, shift = cols[layer][:, v + 1, k:k + 1], cols[layer][:, v, k:k + 1]
                    act.wait_ge(work_full, at + 1)
                    if u >= 4:
                        act.wait_ge(n_lo[n], u - 3)
                    act.activation(hfb[:, u % 4, :], bank[at % WORK][:, :], ACT.Identity, scale=scale, bias=shift)
                    act.activation(h_hi[:, k, u // KB * CH:(u // KB + 1) * CH], bank[at % WORK][:, :], ACT.Identity,
                                   scale=scale, bias=shift).then_inc(work_free, 1)
                    if n % 2 and k == KB - 1 and u // KB >= 2:
                        by_expert_out(u // KB - 2)
                if n % 2:
                    by_expert_out(NC_ - 2)
                    by_expert_out(NC_ - 1)

            def tables():
                act.wait_ge(a_tab, 6)
                for g in range(G0):
                    for r in range(HG):
                        h = g * HG + r
                        act.activation(decay[:, r, g, :], lag[:, :], ACT.Exp, scale=nslope[:, h:h + 1]).then_inc(a_exp, 1)
                for g in range(G0):
                    act.activation(qdec[:, g, :], rowf[:, :], ACT.Exp, scale=nslope_s[:, g:g + 1]).then_inc(a_exp, 1)
                act.activation(kdec[:, :], nslope[:, :], ACT.Exp, scale=endf[:, :]).then_inc(a_exp, 1)
                act.activation(bdec[:, :], nslope_s[:, :], ACT.Exp, scale=float(P)).then_inc(a_exp, 1)

            def linear_attention():
                with act.Fori(0, NC_) as i:
                    work.enter(i, A_WORK)
                    token = lambda t: i * TC + t
                    for g in range(G0):
                        for dst in (qT, kT):
                            at = work.next()
                            act.wait_ge(work_full, at + 1)
                            act.activation(dst[:, g, :], bank[(work.fixed - 1) % WORK][:, :], ACT.Silu).then_inc(a_silu, 1)

                    def by_token(t):
                        at = work.next()
                        act.wait_ge(work_full, at + 1)
                        act.activation(ksil[:, t % 2, :], bank[(work.fixed - 1) % WORK][:, 0:D], ACT.Silu).then_inc(a_ks, 1)
                        work.next()

                    def out_hi(t):
                        at = work.next()
                        act.wait_ge(work_full, at + 1)
                        act.activation(oT_hi[:, t, :], bank[(work.fixed - 1) % WORK][:, 0:D], ACT.Copy).then_inc(a_ohi, 1)

                    by_token(0)
                    for t in range(TC):
                        if t < TC - 1:
                            by_token(t + 1)
                        if t >= 1:
                            out_hi(t - 1)
                        at = work.next()
                        act.wait_ge(work_full, at + 1)
                        act.activation(osq[:, :], bank[(work.fixed - 1) % WORK][:, 0:D], ACT.Square,
                                       accum_out=ssq[:, t:t + 1]).then_inc(a_sq, 1)
                        work.next()
                    out_hi(TC - 1)
                    act.wait_ge(a_sq, i * TC + TC)
                    act.activation(rms[:, :], ssq[:, :], ACT.Sqrt, scale=1.0 / D, bias=eps_rms[:, :]).then_inc(a_std, 1)
                    work.fixed += TC
                work.leave(NC_)

            def mixture(n):
                tiles, T = m_tiles[n], m_count[n]
                nf = len(tiles)
                act.wait_ge(m_top[n], 10)
                act.activation(sc[:, :, :], sc[:, :, :], ACT.Exp).then_inc(m_exp[n], 1)
                tile, hi = Turn(), Turn()

                def expert():
                    for c in range(NC_):
                        def hi_part(f, at):
                            w = tiles[f][1]
                            hi.next()
                            act.wait_ge(work_free, at)
                            act.activation(hid_hi[0:w, (hi.fixed - 1) % HID, :], hid[0:w, (hi.fixed - 1) % 2, :],
                                           ACT.Copy).then_inc(m_hi[n], 1)

                        before = None
                        for f, (f0, w) in enumerate(tiles):
                            tile.next()
                            banks, gate = m_banks[n][f], work.fixed % WORK
                            at = [work.next() for _ in range(banks)][0]
                            row = 0 if banks == 2 else w
                            act.wait_ge(work_full, at + 1)
                            act.wait_ge(work_free, at - m_banks[n][f - 1])
                            act.activation(sil[0:w, (tile.fixed - 1) % 2, :], bank[gate][row:row + w, :],
                                           ACT.Silu).then_inc(m_sil[n], 1)
                            if f:
                                hi_part(f - 1, before)
                            before = work.at()
                        hi_part(nf - 1, before)

                rounds = (T - 1) // 2
                with act.Fori(0, rounds) as i:
                    for turn, per in ((work, sum(m_banks[n]) * NC_), (tile, nf * NC_), (hi, nf * NC_)):
                        turn.enter(i, 2 * per)
                    for half in range(2):
                        expert()
                for turn in (work, tile, hi):
                    turn.leave(rounds)
                for e in range(2 * rounds, T):
                    expert()

            def softmax_attention():
                work_s, pt, z, rows = Turn(), Turn(), Turn(), Turn()

                def projected(hi, scale=1.0):
                    u, b = work_s.next(), bank[(work_s.fixed - 1) % S_RING]
                    src = b[:, :]
                    if len(hi.shape) == 3:
                        src = src.rearrange("p (t h) -> p t h", t=2)
                    act.wait_ge(s_full, u + 1)
                    act.activation(hi, src, ACT.Copy, scale=scale).then_inc(s_hi, 1)

                def keys(j, q):
                    for c in range(NC_):
                        projected(KT_hi[:, c * CH:(c + 1) * CH])
                    yield

                def queries(j, q):
                    projected(QT_hi[:, q % 2, :], DH ** -0.5)
                    yield

                def values(j, q):
                    for t in range(0, NT, 2):
                        projected(V_hi[:, t:t + 2, :])
                        yield

                def scores(j, q):
                    def exp_part(r, half, n0, n1):
                        p = prob[q % 2][:, row_start(q, r) + n0:row_start(q, r) + n1]
                        return act.activation(p, p, ACT.Exp, bias=nmax[:, q, r:r + 1], accum_out=rsum[:, half, q, r:r + 1])

                    parts = [(r, c) for r in range(TC) for c in range(q + 1)]
                    due = {}
                    for r in range(TC):
                        at, width = (r + 1) * (q + 1), row_width(q, r)
                        due.setdefault(at, []).append((r, 0, 0, min(width, EXP_MOST)))
                        if width > EXP_MOST:
                            due.setdefault(at + 1, []).append((r, 1, EXP_MOST, width))
                    for n in range(len(parts) + 2):
                        for r, half, n0, n1 in due.get(n, []):
                            if half == 0:
                                act.wait_ge(s_row, rows.next() + 1)
                            ins = exp_part(r, half, n0, n1)
                            if n1 == row_width(q, r):
                                ins.then_inc(s_exp, 1)
                        if n < len(parts):
                            work_s.fixed += 1
                            yield

                def turned(j, q):
                    for kt in range(TC * (q + 1)):
                        if kt >= AHEAD:
                            yield
                        r0 = max(0, kt - TC * q) * P
                        u, s = pt.next(), kt % PTR
                        act.wait_ge(s_pt, u + 1)
                        act.activation(pT_hi[:, s, r0:CH], bank[S_RING + s][:, r0:CH], ACT.Copy).then_inc(s_phi, 1)
                    for _ in range(AHEAD + 1):
                        yield

                def head_out(j, q):
                    act.wait_ge(s_z, z.next() + 1)
                    act.activation(zT_hi[:, q % 2, :], bank[Z_BANK + q % 2][:, :], ACT.Copy).then_inc(s_zhi, 1)
                    yield

                def outputs(j, q):
                    work_s.fixed += TC // 2
                    yield

                steps = {"K": keys, "Q": queries, "V": values, "S": scores, "T": turned, "Z": head_out, "O": outputs}
                with act.Fori(0, H1 // 2) as i:
                    for turn, per in ((work_s, PAIR_WORK), (pt, 2 * HEAD_PT), (z, 2 * NC_), (rows, 2 * NT)):
                        turn.enter(i, per)
                    for line in ORDER:
                        take(steps, line)
                for turn in (work_s, pt, z, rows):
                    turn.leave(H1 // 2)

            modulation(0)
            act.wait_ge(consts, 8)
            norm(0)
            modulation(1)
            tables()
            linear_attention()
            if stop >= 1:
                norm(1)
                mixture(0)
            if stop >= 2:
                norm(2)
                softmax_attention()
            if stop >= 3:
                norm(3)
                mixture(1)

        @block.tensor
        def _(pe):
            work = Turn()

            def work_bank():
                at = work.next()
                wait(pe, work_free, at + 1 - WORK)
                return bank[(work.fixed - 1) % WORK]

            def three(dst, lhs, rhs, first, last):
                for a, b in ((0, 0), (0, 1), (1, 0)):
                    ins = pe.matmul(dst, lhs[a], rhs[b], start=first and (a, b) == (0, 0),
                                    stop=last and (a, b) == (1, 0), skip_group_check=True)
                return ins

            def modulation(n):
                pe.wait_ge(wmod_loaded, 16 * (n + 1))
                pe.wait_ge(c_silu, n + 1)
                b = work_bank()
                for v, part in enumerate((0, 1, 3, 4)):
                    for k in range(KB):
                        for kk in range(KB):
                            ins = pe.matmul(b[:, v * KB + k:v * KB + k + 1],
                                            wmod[:, kk, part * D + k * P:part * D + (k + 1) * P], csil[:, kk:kk + 1],
                                            start=v + k + kk == 0, stop=kk == KB - 1, skip_group_check=True)
                ins.then_inc(work_full, 1)
                pe.wait_ge(c_wide, KB * (n + 1))
                b = work_bank()
                for g, part in enumerate((2, 5)):
                    for kk in range(KB):
                        ins = pe.matmul(b[:, g * D:(g + 1) * D], cwide[:, kk, :], wmod[:, kk, part * D:(part + 1) * D],
                                        start=g + kk == 0, stop=kk == KB - 1, skip_group_check=True)
                ins.then_inc(work_full, 1)

            def routed(n, c):
                if c == 0:
                    pe.wait_ge(m_top[n], 2)
                if c >= ROUTED:
                    pe.wait_ge(m_sce[n], c - ROUTED + 1)
                pe.wait_ge(n_lo[2 * n + 1], (c + 1) * KB)
                for k in range(KB):
                    ins = three(bank[SIDE + 1 + c % ROUTED][0:E, :], [r[:, k, :] for r in (rt_hi, rt_lo)],
                                [a[:, k, c * CH:(c + 1) * CH] for a in (h_hi, h_lo)], k == 0, k == KB - 1)
                ins.then_inc(m_scr[n], 1)

            def routed_by_token(n, c):
                pe.wait_ge(m_sce[n], c + 1)
                for t in range(TC):
                    ins = pe.transpose(bank[SIDE][:, (c * TC + t) * E:(c * TC + t + 1) * E],
                                       by_expert[0:E, c % 2, t * P:(t + 1) * P], ident[0:E, 0:E])
                ins.then_inc(m_sc[n], 1)

            def norm(n):
                xh, _ = mo(n)
                routes = n % 2
                for c in range(NC_ + 3):
                    if c < NC_:
                        pe.wait_ge(n_xhat[n], (c + 1) * TC)
                        for k in range(KB):
                            b = work_bank()
                            for t in range(TC):
                                ins = pe.transpose(b[:, t * P:(t + 1) * P], xh[:, (c * TC + t) % (2 * TC), k * P:(k + 1) * P], ident[:, :])
                            ins.then_inc(work_full, 1)
                    if routes and 0 <= c - 2 < NC_:
                        routed(n // 2, c - 2)
                    if routes and c >= 3:
                        routed_by_token(n // 2, c - 3)

            def linear_attention():
                pe.wait_ge(n_lo[0], NC_ * KB)
                pe.wait_ge(a_split, 13)
                pe.wait_ge(a_sel, 2)
                with pe.Fori(0, NC_) as i:
                    work.enter(i, A_WORK)
                    token = lambda t: i * TC + t
                    hc = (hc_hi, hc_lo)
                    for g in range(G0):
                        for m in (g, G0 + g):
                            b = work_bank()
                            for k in range(KB):
                                ins = three(b[:, :], [w[:, k, m, :] for w in (wqk_hi, wqk_lo)], 
                                            [h[:, k, bass.ds(i * CH, CH)] for h in (h_hi, h_lo)], k == 0, k == KB - 1)
                            ins.then_inc(work_full, 1)
                    pe.wait_ge(a_hc, i * 2 * KB + 2 * KB)
                    features = work.at()

                    def by_token(t):
                        for c0_, c1_ in ((0, 2 * D), (2 * D, 3 * D)):
                            b = work_bank()
                            for k in range(KB):
                                ins = three(b[:, 0:c1_ - c0_], [h[:, k, t * P:(t + 1) * P] for h in hc],
                                            [w[:, k, c0_:c1_] for w in (wkvu_hi, wkvu_lo)], k == 0, k == KB - 1)
                            ins.then_inc(work_full, 1)
                        return work.at()

                    def turn_out(t, gated):
                        b = work_bank()
                        pe.wait_ge(work_free, gated + 1)
                        for k in range(KB):
                            ins = pe.transpose(b[:, k * P:(k + 1) * P], ou[:, t % 2, k * P:(k + 1) * P], ident[:, :])
                        ins.then_inc(work_full, 1)
                        return work.at()

                    by = by_token(0)
                    gated = lo_done = None
                    for t in range(TC):
                        cut = slice(t * P, (t + 1) * P)
                        pe.wait_ge(work_free, features)
                        for g in range(G0):
                            for r in range(HG):
                                s = slice(r * STRIP, r * STRIP + D0)
                                ins = pe.matmul(bank[SIDE + r][:, g * P:(g + 1) * P], kT[s, g, cut], qT[s, g, cut],
                                                start=g == 0, stop=True, skip_group_check=True)
                                if g == G0 - 1:
                                    ins.then_inc(a_score, 1)
                        nxt = by_token(t + 1) if t < TC - 1 else None
                        if t >= 1:
                            turn_out(t - 1, gated)
                        b = work_bank()
                        gated = work.at() - 1
                        pe.wait_ge(a_kv, token(t) * G0 + G0)
                        for g in range(G0):
                            pe.matmul(b[:, g * HG * D0:(g + 1) * HG * D0], qdT[:, g, cut], kv[:, g, :],
                                      start=g == 0, stop=False, skip_group_check=True)
                        pe.wait_ge(work_free, by)
                        pe.wait_ge(a_mask, token(t) * HG + HG)
                        for g in range(G0):
                            for r in range(HG):
                                h = g * HG + r
                                ins = pe.matmul(b[:, h * D0:(h + 1) * D0], amat[:, r, g, :], vt[:, t % 2, h * D0:(h + 1) * D0],
                                                start=False, stop=True, skip_group_check=True)
                        ins.then_inc(work_full, 1)
                        b = work_bank()
                        pe.wait_ge(a_kd, token(t) + 1)
                        for g in range(G0):
                            ins = pe.matmul(b[:, g * HG * D0:(g + 1) * HG * D0], kd[:, t % 2, g * HG:(g + 1) * HG, :].rearrange("p r s -> p (r s)"),
                                            vt[:, t % 2, g * HG * D0:(g + 1) * HG * D0], start=g == 0, stop=True, skip_group_check=True)
                        ins.then_inc(work_full, 1)
                        by = nxt
                    split_at = turn_out(TC - 1, gated)
                    for t in range(TC):
                        b = work_bank()
                        if t == 0:
                            pe.wait_ge(work_free, split_at)
                        for k in range(KB):
                            ins = three(b[:, 0:D], [o[:, t, k * P:(k + 1) * P] for o in (oT_hi, oT_lo)],
                                        [w[:, k, :] for w in (wo0_hi, wo0_lo)], k == 0, k == KB - 1)
                        ins.then_inc(work_full, 1)
                work.leave(NC_)

            def mixture(n):
                F, tiles, T = F_L[n], m_tiles[n], m_count[n]
                nf = len(tiles)
                h = (h_hi, h_lo)
                tile, y = Turn(), Turn()

                def front(e, half, c):
                    if c == 0:
                        pe.wait_ge(m_raw[n], e * 5 + 2)
                    for (f0, w), banks in zip(tiles, m_banks[n]):
                        m = 2 * w // banks
                        for at in range(2 * f0, 2 * (f0 + w), m):
                            b = work_bank()
                            for k in range(KB):
                                ins = three(b[0:m, :], [a[:, k, at:at + m] for a in (gu_hi[half], gu_lo[half])],
                                            [a[:, k, c * CH:(c + 1) * CH] for a in h], k == 0, k == KB - 1)
                            ins.then_inc(work_full, 1)

                def back(e, half, c):
                    if c == 0:
                        pe.wait_ge(m_raw[n], e * 5 + 5)
                    banks = []
                    for _ in range(2):
                        y.next()
                        banks.append(bank[SIDE + (y.fixed - 1) % 4])
                    pe.wait_ge(m_top[n], 3)
                    for f in range(nf):
                        pe.wait_ge(m_lo[n], tile.next() + 1)
                        s = (tile.fixed - 1) % HID
                        for t in range(TC):
                            ins = three(banks[t // 2][:, t % 2 * D:(t % 2 + 1) * D],
                                        [a[:, s, t * P:(t + 1) * P] for a in (hid_hi, hid_lo)],
                                        [a[:, f, :] for a in (dn_hi[half], dn_lo[half])], f == 0 and t % 2 == 0, f == nf - 1)
                            if f == nf - 1 and t % 2:
                                ins.then_inc(m_y[n], 1)

                rounds = (T - 1) // 2
                if LEAD[n]:
                    front(0, 0, 0)
                with pe.Fori(0, rounds) as i:
                    for turn, per in ((work, sum(m_banks[n]) * NC_), (tile, nf * NC_), (y, 2 * NC_)):
                        turn.enter(i, 2 * per)
                    units(n, [(2 * i + half, half, True) for half in range(2)], front, back)
                for turn in (work, tile, y):
                    turn.leave(rounds)
                units(n, [(e, e % 2, e < T - 1) for e in range(2 * rounds, T)], front, back)

            def softmax_attention():
                work_s, pt, z, rows = Turn(), Turn(), Turn(), Turn()
                h = (h_hi, h_lo)
                pe.wait_ge(n_lo[2], NC_ * KB)
                key_at, query_at, value_at, rows_at, z_at = {}, {}, {}, {}, {}

                def ring():
                    at = work_s.next()
                    pe.wait_ge(s_free, at + 1)
                    return bank[(work_s.fixed - 1) % S_RING]

                def read(at):
                    pe.wait_ge(s_free, at + 1 + S_RING)

                def keys(j, q):
                    pe.wait_ge(s_split, rounds_of(PAIR_SPLIT) + 4 + 2 * j)
                    for c in range(NC_):
                        b = ring()
                        for k in range(KB):
                            ins = three(b[:, :], [w[:, k, 2 * j * DH:(2 * j + 1) * DH] for w in (wkq_hi, wkq_lo)],
                                        [a[:, k, c * CH:(c + 1) * CH] for a in h], k == 0, k == KB - 1)
                        ins.then_inc(s_full, 1)
                    key_at[j] = work_s.at() - 1
                    yield

                def queries(j, q):
                    if q == 0:
                        pe.wait_ge(s_split, rounds_of(PAIR_SPLIT) + 4 + 2 * j)
                    b = ring()
                    query_at[j, q] = work_s.at() - 1
                    for k in range(KB):
                        ins = three(b[:, :], [w[:, k, (2 * j + 1) * DH:(2 * j + 2) * DH] for w in (wkq_hi, wkq_lo)],
                                    [a[:, k, q * CH:(q + 1) * CH] for a in h], k == 0, k == KB - 1)
                    ins.then_inc(s_full, 1)
                    yield

                def values(j, q):
                    pe.wait_ge(s_split, rounds_of(PAIR_SPLIT) + 2)
                    for t in range(NT):
                        if t % 2 == 0:
                            b = ring()
                        for k in range(KB):
                            ins = three(b[:, t % 2 * 2 * DH:(t % 2 + 1) * 2 * DH], [a[:, k, t * P:(t + 1) * P] for a in h],
                                        [w[:, k, :] for w in (wv_hi, wv_lo)], t % 2 == 0 and k == 0, k == KB - 1)
                        if t % 2:
                            ins.then_inc(s_full, 1)
                            value_at[0] = work_s.at() - 1
                            yield

                def scores(j, q):
                    later = max(IN_ORDER.index(("Q", j, q)), IN_ORDER.index(("K", j, 0)))
                    read(query_at[j, q] if IN_ORDER[later][0] == "Q" else key_at[j])
                    for r in range(TC):
                        for c in range(q + 1):
                            b = ring()
                            n = CH if c < q else (r + 1) * P
                            three(b[:, 0:n], [a[:, q % 2, r * P:(r + 1) * P] for a in (QT_hi, QT_lo)],
                                  [a[:, c * CH:c * CH + n] for a in (KT_hi, KT_lo)], True, True).then_inc(s_full, 1)
                            if c == q:
                                rows.next()
                                rows_at[j, q, r] = rows.at()
                            yield

                def turn(j, q, kt, s):
                    p = prob[q % 2]
                    for r in range(max(0, kt - TC * q), TC):
                        if kt == 0:
                            pe.wait_ge(s_exp, rows_at[j, q, r])
                        at0 = row_start(q, r) + kt * P
                        ins = pe.transpose(bank[S_RING + s][:, r * P:(r + 1) * P], p[:, at0:at0 + P], ident[:, :])
                    ins.then_inc(s_pt, 1)

                def turned(j, q):
                    count, ahead = TC * (q + 1), AHEAD
                    for kt in range(min(ahead, count)):
                        turn(j, q, kt, kt % PTR)
                    yield
                    if q == 0:
                        read(value_at[0])
                    for kt in range(count):
                        s, r0 = kt % PTR, max(0, kt - TC * q) * P
                        pe.wait_ge(s_plo, pt.next() + 1)
                        ins = three(bank[Z_BANK + q % 2][:, r0:CH], [a[:, kt, j * DH:(j + 1) * DH] for a in (V_hi, V_lo)],
                                    [a[:, s, r0:CH] for a in (pT_hi, pT_lo)], kt == 0, kt == count - 1)
                        if kt + ahead < count:
                            turn(j, q, kt + ahead, (kt + ahead) % PTR)
                        if kt == count - 1:
                            ins.then_inc(s_z, 1)
                            z.next()
                            z_at[j, q] = z.at()
                        yield

                def head_out(j, q):
                    yield

                def outputs(j, q):
                    if j == 0 and q == 0:
                        pe.wait_ge(s_split, rounds_of(PAIR_SPLIT) + PAIR_SPLIT)
                    for t in range(TC):
                        if t % 2 == 0:
                            b = ring()
                        if t == 0:
                            pe.wait_ge(s_zlo, z_at[j, q])
                        ins = three(b[:, t % 2 * D:(t % 2 + 1) * D], [a[:, q % 2, t * P:(t + 1) * P] for a in (zT_hi, zT_lo)],
                                    [w[:, j, :] for w in (wo_hi, wo_lo)], t % 2 == 0, True)
                        if t % 2:
                            ins.then_inc(s_full, 1)
                    yield

                steps = {"K": keys, "Q": queries, "V": values, "S": scores, "T": turned, "Z": head_out, "O": outputs}
                with pe.Fori(0, H1 // 2) as i:
                    rounds_of = lambda per: i * per
                    for turn_, per in ((work_s, PAIR_WORK), (pt, 2 * HEAD_PT), (z, 2 * NC_), (rows, 2 * NT)):
                        turn_.enter(i, per)
                    for line in ORDER:
                        take(steps, line)
                for turn_ in (work_s, pt, z, rows):
                    turn_.leave(H1 // 2)

            modulation(0)
            norm(0)
            modulation(1)
            linear_attention()
            if stop >= 1:
                norm(1)
                mixture(0)
            if stop >= 2:
                norm(2)
                softmax_attention()
            if stop >= 3:
                norm(3)
                mixture(1)


def arrays_of(inputs):
    import numpy as np

    def a(name):
        return np.asarray(inputs[name])

    def by_tile(gate_up):
        gate, up = np.split(gate_up, 2, axis=-1)
        tiles = [slice(f, min(f + 128, gate.shape[-1])) for f in range(0, gate.shape[-1], 128)]
        return np.concatenate([part for t in tiles
                               for part in ((gate[..., t], up[..., t]), (up[..., t], gate[..., t]))[2 * (t.stop - t.start) <= 128]],
                              axis=-1)

    d = a("L0_attn_x").shape[-1]
    qkvu = a("L0_attn_W_qkvu").T
    lay = {
        "x": a("L0_attn_x")[0],
        "slope": a("L0_attn_slope_rate"),
        "w_qk": qkvu[:, 0:2 * d],
        "w_kvu": qkvu[:, d:],
        "w_out0": a("L0_attn_W_out").T,
        "router0": a("L0_ffn_w_gate_router").T,
        "gu0": by_tile(np.concatenate([a("L0_ffn_w_gate_proj"), a("L0_ffn_w_up_proj")], axis=1).transpose(0, 2, 1)),
        "down0": a("L0_ffn_w_down_proj").transpose(0, 2, 1),
        "c0": a("L0_c").reshape(-1, 128).T,
        "wmod0": a("L0_wmod"),
        "w_k": a("L1_attn_W_K").transpose(0, 2, 1),
        "w_q": a("L1_attn_W_Q").transpose(0, 2, 1),
        "w_v": a("L1_attn_W_V").transpose(0, 2, 1),
        "w_o": a("L1_attn_W_O").reshape(d, a("L1_attn_W_K").shape[0], -1).transpose(1, 2, 0),
        "router1": a("L1_ffn_gate_w").T,
        "gu1": by_tile(np.concatenate([a("L1_ffn_expert_gate_up"), a("L1_ffn_base_gate_up")[None]])),
        "down1": np.concatenate([a("L1_ffn_expert_down"), a("L1_ffn_base_down")[None]]),
        "c1": a("L1_c").reshape(-1, 128).T,
        "wmod1": a("L1_wmod"),
    }
    return {k: np.ascontiguousarray(v) for k, v in lay.items()}


def kernel(**inputs):
    import concourse.bacc as bacc
    import numpy as np
    from concourse.bass_utils import run_bass_kernel_spmd

    nc = bacc.Bacc("TRN2", target_bir_lowering=False, num_devices=1)
    arrays, args = {}, []
    for name, a in arrays_of(inputs).items():
        arrays[f"in_{name}_dram"] = a
        args.append(nc.dram_tensor(f"in_{name}_dram", a.shape, mybir.dt.from_np(a.dtype), kind="ExternalInput").ap())
    shape = arrays["in_x_dram"].shape
    args.append(nc.dram_tensor("out_0_dram", shape, F32, kind="ExternalOutput").ap())
    two_blocks(nc, *args)
    r = run_bass_kernel_spmd(nc, [arrays], core_ids=[0])
    return np.asarray(r.results[0]["out_0_dram"]).reshape(1, *shape)
```
